# Optimizing a Trainium2 kernel written in Bass

```python
import numpy as np
import jax
import jax.numpy as jnp

def _softmax(x, axis=-1):
    return jax.nn.softmax(x, axis=axis)

def _gelu(x):
    return jax.nn.gelu(x, approximate=True)

def _silu(x):
    return jax.nn.silu(x)

def _sigmoid(x):
    return jax.nn.sigmoid(x)

def _layernorm(x, axis=-1, eps=1e-05):
    m = jnp.mean(x, axis=axis, keepdims=True)
    v = jnp.var(x, axis=axis, keepdims=True)
    return (x - m) / jnp.sqrt(v + eps)

def _scatter_add(tgt, idx, src, axis=0):
    return tgt.at[idx].add(src)

def _segment_sum(src, seg, n):
    return jax.ops.segment_sum(src, seg, n)
kernel_name = 'mk_gnn_resnorm_d2_gnn_r8_920a73'

def setup_inputs(seed: int=0):
    np.random.seed(seed)
    _w = jnp.asarray

    def _rec_inputs():
        import jax
        import jax.numpy as jnp
        _gk = jax.random.key(seed)
        x = -1.686e-05 + 1 * jax.random.normal(jax.random.fold_in(_gk, 1), (6250, 160), jnp.float32)
        src = jax.random.randint(jax.random.fold_in(_gk, 2), (200000,), 0, 6250, jnp.int32)
        dst = jnp.minimum((6250 * jax.random.uniform(jax.random.fold_in(_gk, 3), (200000,)) ** 2.0).astype(jnp.int32), 49999)
        _o = jnp.argsort(dst, stable=True)
        src = src[_o]
        dst = dst[_o]
        edge_attr_10 = jax.random.uniform(jax.random.fold_in(_gk, 12), (200000, 10), jnp.float32, 0.0, 1)
        edge_attr_4 = -0.000107899 + 1.00008 * jax.random.normal(jax.random.fold_in(_gk, 13), (200000, 4), jnp.float32)
        node_vec1 = jax.random.uniform(jax.random.fold_in(_gk, 15), (6250, 1), jnp.float32, 0.0, 1)
        return (x, src, dst, edge_attr_10, edge_attr_4, node_vec1)
    x, src, dst, edge_attr_10, edge_attr_4, node_vec1 = _rec_inputs()

    def _L0_gnn_setup():
        import jax, jax.numpy as jnp
        import numpy as np
        N, E = (6250, 100000)
        MUL0, MUL1 = (64, 32)
        D = MUL0 + 3 * MUL1
        INV3 = float(1.0 / np.sqrt(3.0))
        INV6 = float(1.0 / np.sqrt(6.0))
        C0 = float(1.0 / np.sqrt(MUL0 + MUL1))
        C1 = float(np.sqrt(3.0 / (MUL0 + 2 * MUL1)))
        LIN_S = float(1.0 / np.sqrt(MUL0))
        LIN_V = float(1.0 / np.sqrt(MUL1))
        key = jax.random.key(seed)
        ks = jax.random.split(key, 10)
        x = jax.random.normal(ks[0], (N, D), dtype=jnp.float32)
        sh = jax.random.normal(ks[1], (E, 4), dtype=jnp.float32)
        edge_index = jax.random.randint(ks[2], (2, E), 0, N, dtype=jnp.int64)
        W1 = jax.random.normal(ks[3], (MUL0, MUL0), dtype=jnp.float32)
        W2 = jax.random.normal(ks[4], (MUL1, MUL0), dtype=jnp.float32)
        W3 = jax.random.normal(ks[5], (MUL0, MUL1), dtype=jnp.float32)
        W4 = jax.random.normal(ks[6], (MUL1, MUL1), dtype=jnp.float32)
        W5 = jax.random.normal(ks[7], (MUL1, MUL1), dtype=jnp.float32)
        Ws = jax.random.normal(ks[8], (MUL0, MUL0), dtype=jnp.float32)
        Wv = jax.random.normal(ks[9], (MUL1, MUL1), dtype=jnp.float32)
        return {'x': x, 'sh': sh, 'W1': W1, 'W2': W2, 'W3': W3, 'W4': W4, 'W5': W5, 'Ws': Ws, 'Wv': Wv, 'edge_index': edge_index}
    _L0_gnn_all = _L0_gnn_setup()
    _L0_gnn_in = {k: v for k, v in _L0_gnn_all.items() if k in ('W1', 'W2', 'W3', 'W4', 'W5', 'Ws', 'Wv')}
    del _L0_gnn_all

    def _L1_gnn_setup():
        import jax, jax.numpy as jnp
        import numpy as np
        N_NODES = 6250
        N_EDGES = 100000
        MUL0, MUL1 = (64, 32)
        N_BASIS, N_RADIAL = (10, 100)
        W_NUMEL = 192
        NUM_NEIGHBORS = 16.0
        INV_SQRT3 = np.float32(1.0 / np.sqrt(3.0))
        RELU_GAIN = np.float32(np.sqrt(2.0))
        FAN_L2 = np.float32(np.sqrt(MUL0 + MUL1))

        def _fctp_scalar_attr(x0, x1, a, W0, W1):
            o0 = x0 @ W0 * a * (1.0 / np.sqrt(W0.shape[0]))
            o1 = jnp.einsum('nud,uw->nwd', x1, W1) * a[..., None] * (1.0 / np.sqrt(W1.shape[0]))
            return (o0, o1)
        key = jax.random.key(seed)
        ks = jax.random.split(key, 16)
        return {'node_input': jax.random.normal(ks[0], (N_NODES, MUL0 + 3 * MUL1), jnp.float32), 'node_attr': jnp.ones((N_NODES, 1), jnp.float32), 'edge_attr': jax.random.normal(ks[1], (N_EDGES, 4), jnp.float32), 'edge_length_embedded': jax.random.uniform(ks[2], (N_EDGES, N_BASIS), dtype=jnp.float32), 'W_si0': jax.random.normal(ks[3], (MUL0, MUL0), jnp.float32), 'W_si1': jax.random.normal(ks[4], (MUL1, MUL1), jnp.float32), 'W_l1_0': jax.random.normal(ks[5], (MUL0, MUL0), jnp.float32), 'W_l1_1': jax.random.normal(ks[6], (MUL1, MUL1), jnp.float32), 'W_l2_00': jax.random.normal(ks[7], (MUL0, MUL0), jnp.float32), 'W_l2_10': jax.random.normal(ks[8], (MUL1, MUL0), jnp.float32), 'W_l2_01': jax.random.normal(ks[9], (MUL0, MUL1), jnp.float32), 'W_l2_11': jax.random.normal(ks[10], (MUL1, MUL1), jnp.float32), 'W_fc1': jax.random.normal(ks[11], (N_BASIS, N_RADIAL), jnp.float32), 'W_fc2': jax.random.normal(ks[12], (N_RADIAL, W_NUMEL), jnp.float32), 'edge_src': jax.random.randint(ks[13], (N_EDGES,), 0, N_NODES), 'edge_dst': jax.random.randint(ks[14], (N_EDGES,), 0, N_NODES)}
    _L1_gnn_all = _L1_gnn_setup()
    _L1_gnn_in = {k: v for k, v in _L1_gnn_all.items() if k in ('W_si0', 'W_si1', 'W_l1_0', 'W_l1_1', 'W_l2_00', 'W_l2_10', 'W_l2_01', 'W_l2_11', 'W_fc1', 'W_fc2')}
    del _L1_gnn_all
    return {'x': x, 'src': src, 'dst': dst, 'edge_attr_10': edge_attr_10, 'edge_attr_4': edge_attr_4, 'node_vec1': node_vec1, 'L0_gnn_W1': _L0_gnn_in['W1'], 'L0_gnn_W2': _L0_gnn_in['W2'], 'L0_gnn_W3': _L0_gnn_in['W3'], 'L0_gnn_W4': _L0_gnn_in['W4'], 'L0_gnn_W5': _L0_gnn_in['W5'], 'L0_gnn_Ws': _L0_gnn_in['Ws'], 'L0_gnn_Wv': _L0_gnn_in['Wv'], 'L1_gnn_W_si0': _L1_gnn_in['W_si0'], 'L1_gnn_W_si1': _L1_gnn_in['W_si1'], 'L1_gnn_W_l1_0': _L1_gnn_in['W_l1_0'], 'L1_gnn_W_l1_1': _L1_gnn_in['W_l1_1'], 'L1_gnn_W_l2_00': _L1_gnn_in['W_l2_00'], 'L1_gnn_W_l2_10': _L1_gnn_in['W_l2_10'], 'L1_gnn_W_l2_01': _L1_gnn_in['W_l2_01'], 'L1_gnn_W_l2_11': _L1_gnn_in['W_l2_11'], 'L1_gnn_W_fc1': _L1_gnn_in['W_fc1'], 'L1_gnn_W_fc2': _L1_gnn_in['W_fc2']}

def reference(x, src, dst, edge_attr_10, edge_attr_4, node_vec1, L0_gnn_W1, L0_gnn_W2, L0_gnn_W3, L0_gnn_W4, L0_gnn_W5, L0_gnn_Ws, L0_gnn_Wv, L1_gnn_W_si0, L1_gnn_W_si1, L1_gnn_W_l1_0, L1_gnn_W_l1_1, L1_gnn_W_l2_00, L1_gnn_W_l2_10, L1_gnn_W_l2_01, L1_gnn_W_l2_11, L1_gnn_W_fc1, L1_gnn_W_fc2):
    import jax
    import jax.numpy as jnp

    def _L0_gnn_ref(x, sh, W1, W2, W3, W4, W5, Ws, Wv, edge_index):
        import jax, jax.numpy as jnp
        import numpy as np
        N, E = (6250, 100000)
        MUL0, MUL1 = (64, 32)
        D = MUL0 + 3 * MUL1
        INV3 = float(1.0 / np.sqrt(3.0))
        INV6 = float(1.0 / np.sqrt(6.0))
        C0 = float(1.0 / np.sqrt(MUL0 + MUL1))
        C1 = float(np.sqrt(3.0 / (MUL0 + 2 * MUL1)))
        LIN_S = float(1.0 / np.sqrt(MUL0))
        LIN_V = float(1.0 / np.sqrt(MUL1))
        n = x.shape[0]
        src, dst = (edge_index[0], edge_index[1])
        s = x[:, :MUL0]
        v = x[:, MUL0:].reshape(n, MUL1, 3)
        ss, vv = (s[src], v[src])
        e0 = sh[:, 0:1]
        e1 = sh[:, 1:4]
        dot = jnp.einsum('eui,ei->eu', vv, e1)
        out0 = C0 * (ss * e0 @ W1 + dot * INV3 @ W2)
        p3 = (ss @ W3)[:, :, None] * e1[:, None, :] * INV3
        p4 = jnp.einsum('eui,uw->ewi', vv * e0[:, :, None], W4) * INV3
        p5 = jnp.einsum('eui,uw->ewi', jnp.cross(vv, e1[:, None, :]), W5) * INV6
        out1 = C1 * (p3 + p4 + p5)
        m = jnp.concatenate([out0, out1.reshape(-1, 3 * MUL1)], axis=1)
        m_agg = jax.ops.segment_sum(m, dst, num_segments=n)
        hs = m_agg[:, :MUL0] @ Ws * LIN_S
        hv = jnp.einsum('nui,uw->nwi', m_agg[:, MUL0:].reshape(n, MUL1, 3), Wv) * LIN_V
        h = jnp.concatenate([hs, hv.reshape(n, 3 * MUL1)], axis=1)
        return x + jax.nn.relu(h)

    def _L1_gnn_ref(node_input, node_attr, edge_src, edge_dst, edge_attr, edge_length_embedded, W_si0, W_si1, W_l1_0, W_l1_1, W_l2_00, W_l2_10, W_l2_01, W_l2_11, W_fc1, W_fc2):
        import jax, jax.numpy as jnp
        import numpy as np
        N_NODES = 6250
        N_EDGES = 100000
        MUL0, MUL1 = (64, 32)
        N_BASIS, N_RADIAL = (10, 100)
        W_NUMEL = 192
        NUM_NEIGHBORS = 16.0
        INV_SQRT3 = np.float32(1.0 / np.sqrt(3.0))
        RELU_GAIN = np.float32(np.sqrt(2.0))
        FAN_L2 = np.float32(np.sqrt(MUL0 + MUL1))

        def _fctp_scalar_attr(x0, x1, a, W0, W1):
            o0 = x0 @ W0 * a * (1.0 / np.sqrt(W0.shape[0]))
            o1 = jnp.einsum('nud,uw->nwd', x1, W1) * a[..., None] * (1.0 / np.sqrt(W1.shape[0]))
            return (o0, o1)
        N = node_input.shape[0]
        x0 = node_input[:, :MUL0]
        x1 = node_input[:, MUL0:].reshape(N, MUL1, 3)
        a = node_attr
        h = jax.nn.relu(edge_length_embedded @ W_fc1 * (1.0 / np.sqrt(N_BASIS))) * RELU_GAIN
        w = h @ W_fc2 * (1.0 / np.sqrt(N_RADIAL))
        w0, w1, w2, w3 = (w[:, :64], w[:, 64:128], w[:, 128:160], w[:, 160:192])
        si0, si1 = _fctp_scalar_attr(x0, x1, a, W_si0, W_si1)
        l0, l1 = _fctp_scalar_attr(x0, x1, a, W_l1_0, W_l1_1)
        y0 = l0[edge_src]
        y1 = l1[edge_src]
        e0 = edge_attr[:, :1]
        e1 = edge_attr[:, 1:4]
        m0 = w0 * y0 * e0
        m1 = (w1 * y0)[:, :, None] * e1[:, None, :]
        m2 = (w2 * e0)[:, :, None] * y1
        m3 = w3 * jnp.einsum('eud,ed->eu', y1, e1) * INV_SQRT3
        inv = np.float32(1.0 / np.sqrt(NUM_NEIGHBORS))
        s0 = jax.ops.segment_sum(m0, edge_dst, num_segments=N) * inv
        s1 = jax.ops.segment_sum(m1, edge_dst, num_segments=N) * inv
        s2 = jax.ops.segment_sum(m2, edge_dst, num_segments=N) * inv
        s3 = jax.ops.segment_sum(m3, edge_dst, num_segments=N) * inv
        o0 = (s0 @ W_l2_00 + s3 @ W_l2_10) * a / FAN_L2
        o1 = (jnp.einsum('nud,uw->nwd', s1, W_l2_01) + jnp.einsum('nud,uw->nwd', s2, W_l2_11)) * a[..., None] / FAN_L2
        out0 = si0 + 0.5 * o0
        out1 = si1 + 0.5 * o1
        return jnp.concatenate([out0, out1.reshape(N, 3 * MUL1)], axis=1)
    edge_index = jnp.stack([src, dst])
    x = _layernorm(x + _L0_gnn_ref(x, edge_attr_4, L0_gnn_W1, L0_gnn_W2, L0_gnn_W3, L0_gnn_W4, L0_gnn_W5, L0_gnn_Ws, L0_gnn_Wv, edge_index), axis=-1)
    x = _layernorm(x + _L1_gnn_ref(x, node_vec1, src, dst, edge_attr_4, edge_attr_10, L1_gnn_W_si0, L1_gnn_W_si1, L1_gnn_W_l1_0, L1_gnn_W_l1_1, L1_gnn_W_l2_00, L1_gnn_W_l2_10, L1_gnn_W_l2_01, L1_gnn_W_l2_11, L1_gnn_W_fc1, L1_gnn_W_fc2), axis=-1)
    return x

_drawn_inputs = setup_inputs


def setup_inputs(seed=0):
    import zlib

    import numpy as np

    out = dict(_drawn_inputs(seed))
    spreads = {}
    factors = {}
    for name, (base, spread) in spreads.items():
        noise = np.random.default_rng([zlib.crc32(name.encode()), seed]).standard_normal(out[name].shape)
        drawn = base * np.exp(spread * noise) if base else spread * noise
        out[name] = jnp.asarray(drawn.astype(out[name].dtype))
    for name, factor in factors.items():
        out[name] = (out[name] * factor).astype(out[name].dtype)
    return out
```

```python
from contextlib import ExitStack

import numpy as np

import concourse.bass as bass
from concourse import mybir

F32 = mybir.dt.float32
I32 = mybir.dt.int32
ALU = mybir.AluOpType
ACT = mybir.ActivationFunctionType
AX = mybir.AxisListType
DVE = mybir.EngineType.DVE

P = 128
N, E = 6250, 200000
MUL0, MUL1 = 64, 32
D = MUL0 + 3 * MUL1
NB, NR = 10, 100
NW = 2 * MUL0 + 2 * MUL1
NT = -(-N // P)
NPAD = NT * P
K = 3
BE = K * P
W = 32
U = 6
H = U // 2 * K
ITERS = -(-E // (BE * U))
BLOCKS = ITERS * U
TILES = BLOCKS * K
EPAD = TILES * P
FW = P

EPS = 1e-5
C0 = 1.0 / np.sqrt(MUL0 + MUL1)
C1 = np.sqrt(3.0 / (MUL0 + 2 * MUL1))
INV3, INV6 = 1.0 / np.sqrt(3.0), 1.0 / np.sqrt(6.0)
LIN_S, LIN_V = 1.0 / np.sqrt(MUL0), 1.0 / np.sqrt(MUL1)
RELU_SCALE = float(np.sqrt(2.0) / np.sqrt(NB))
SUM_SCALE = float(0.5 / np.sqrt(MUL0 + MUL1) / np.sqrt(16.0) / np.sqrt(NR))


def build(nc, a, out):
    ctx = ExitStack()
    with ctx:
        def sb(name, shape, dt=F32):
            return ctx.enter_context(nc.sbuf_tensor(name, shape, dt))

        def psum(name, shape):
            return ctx.enter_context(nc.psum_tensor(name, shape, F32))

        def sem(name):
            return ctx.enter_context(nc.semaphore(name))

        def dram(name, shape, dt=F32):
            return nc.dram_tensor(name, shape, dt).ap()

        acc_a = sb("acc_a", [P, 4, NPAD])
        acc_b = sb("acc_b", [P, NPAD])
        sh = sb("sh", [P, TILES, 4])
        rel = sb("rel", [P, TILES])
        iota = sb("iota", [P, W])
        ident = sb("ident", [P, P])
        base_row = sb("base_row", [1, BLOCKS], I32)
        flag = sb("flag", [1, 1], I32)
        node_attr = sb("node_attr", [P, NT])
        msg_w = sb("msg_w", [P, 5, D])
        lin_w = sb("lin_w", [P, 2, P])
        lin_wz = sb("lin_wz", [MUL1, 2, MUL1])
        sum_w = sb("sum_w", [P, 5, D])
        fc1 = sb("fc1", [NB, NR])
        fc2 = sb("fc2", [NR, NW])
        idx = [sb(f"idx{h}", [P, H], I32) for h in range(2)]
        eps = sb("eps", [P, 1])

        work = sb("work", [P, 11000])
        used = [0]

        def carve(cols, parts=P):
            lo = used[0]
            used[0] += cols
            assert used[0] <= 11000
            return work[0:parts, lo:lo + cols]

        gat = [carve(K * D).rearrange("p (k d) -> p k d", k=K) for _ in range(U)]
        hot = [carve(K * 5 * W).rearrange("p (k j n) -> p k j n", k=K, j=5) for _ in range(2)]
        prod = [carve(K * 256).rearrange("p (k d) -> p k d", k=K) for _ in range(2)]
        edge_y = [carve(K * D).rearrange("p (k d) -> p k d", k=K) for _ in range(2)]
        dot3 = carve(K * 96).rearrange("p (k i u) -> p k i u", k=K, i=3)
        dot = carve(K * MUL1).rearrange("p (k u) -> p k u", k=K)
        hid = [carve(BE, NR) for _ in range(2)]
        rad = [carve(BE, NB) for _ in range(U)]

        psum_all = psum("psum_all", [P, 8, 512])
        banks = [psum_all[:, n, :] for n in range(8)]

        base_dram = dram("base_dram", [BLOCKS], I32)
        far_dram = dram("far_dram", [P], F32)
        y_dram = dram("y_dram", [NPAD, D])
        pre_dram = dram("pre_dram", [NPAD, D])

        w1t, ws, w2t = work[0:64, 0:64], work[0:64, 64:128], work[0:64, 128:256]
        w3t, wv, w4t, w5t = work[0:32, 256:320], work[0:32, 320:352], work[0:32, 352:480], work[0:32, 480:608]
        dst_rows = work[0:ITERS, 608:608 + U * BE].rearrange("p (b e) -> p b e", b=U)
        bmin = work[0:ITERS, 3000:3000 + U]
        bmin_i = work[0:ITERS, 3010:3010 + U].bitcast(I32)
        base_b = work[:, 3020:3020 + BLOCKS].bitcast(I32)
        far = work[:, 4080:4081]
        far_row = work[0:1, 4100:4100 + P]
        far_max = work[0:1, 4230:4231]
        weights_loaded, places_loaded, dst_loaded, tables_loaded = (
            sem("weights_loaded"), sem("places_loaded"), sem("dst_loaded"), sem("tables_loaded"))
        zeroed, bases_found, bases_stored, bases_loaded = (
            sem("zeroed"), sem("bases_found"), sem("bases_stored"), sem("bases_loaded"))
        far_found, far_stored, far_loaded = sem("far_found"), sem("far_stored"), sem("far_loaded")
        products_done, setup_step, ident_done = sem("products_done"), sem("setup_step"), sem("ident_done")

        with nc.Block() as block:
            @block.sync
            def _(sp):
                sp.dma_start(dst_rows.bitcast(I32), a["dst"].rearrange("(p b e) -> p b e", p=ITERS, b=U)).then_inc(dst_loaded, 16)
                sp.dma_start(rel[:].bitcast(I32), a["dst_tiles"]).then_inc(tables_loaded, 16)
                for dst, src in ((w1t, a["W1t"]), (ws, a["Ws"]), (w3t, a["W3t"]), (wv, a["Wv"])):
                    sp.dma_start(dst, src).then_inc(weights_loaded, 16)
                for r in range(4):
                    for dst, src in ((w2t, a["W2t"]), (w4t, a["W4t"]), (w5t, a["W5t"])):
                        sp.dma_start(dst[:, 32 * r:32 * r + 32], src).then_inc(weights_loaded, 16)
                sp.dma_start(sh[:], a["sh"]).then_inc(tables_loaded, 16)
                sp.dma_start(node_attr[:], a["node_attr"]).then_inc(tables_loaded, 16)
                sp.dma_start(fc1[:], a["fc1"]).then_inc(tables_loaded, 16)
                sp.dma_start(fc2[:], a["fc2"]).then_inc(tables_loaded, 16)
                sp.wait_ge(bases_found, 1)
                sp.dma_start(base_dram.rearrange("(p b) -> p b", p=ITERS), bmin_i).then_inc(bases_stored, 16)
                sp.wait_ge(bases_stored, 16)
                sp.dma_start(base_b, base_dram.rearrange("(o b) -> o b", o=1).to_broadcast([P, BLOCKS])).then_inc(bases_loaded, 16)
                sp.dma_start(base_row[:], base_dram.rearrange("(o b) -> o b", o=1)).then_inc(bases_loaded, 16)
                sp.wait_ge(zeroed, 1)
                for n, (s, v) in enumerate((("W_l1_0", "W_l1_1"), ("W_si0", "W_si1"))):
                    sp.dma_start(lin_w[0:64, n, 0:64], a[s]).then_inc(places_loaded, 16)
                    sp.dma_start(lin_w[64:96, n, 64:96], a[v]).then_inc(places_loaded, 16)
                    sp.dma_start(lin_w[96:128, n, 96:128], a[v]).then_inc(places_loaded, 16)
                    sp.dma_start(lin_wz[:, n, :], a[v]).then_inc(places_loaded, 16)
                sp.dma_start(sum_w[0:64, 0, 0:64], a["W_l2_00"]).then_inc(places_loaded, 16)
                for i in range(3):
                    lo = MUL0 + MUL1 * i
                    sp.dma_start(sum_w[64:128, 1 + i, lo:lo + 32], a["W_l2_01"]).then_inc(places_loaded, 16)
                    sp.dma_start(sum_w[32 * i:32 * i + 32, 4, lo:lo + 32], a["W_l2_11"]).then_inc(places_loaded, 16)
                sp.dma_start(sum_w[96:128, 4, 0:64], a["W_l2_10"]).then_inc(places_loaded, 16)
                sp.wait_ge(far_found, 1)
                sp.dma_start(far_dram.rearrange("(p o) -> p o", o=1), far).then_inc(far_stored, 16)
                sp.wait_ge(far_stored, 16)
                sp.dma_start(far_row, far_dram.rearrange("(o p) -> o p", o=1)).then_inc(far_loaded, 16)

            WEIGHTS, PLACES, TABLES = 16 * 16, 16 * 16, 16 * 5

            @block.gpsimd
            def _(pool):
                pool.memset(ident[:], 0.0).then_inc(ident_done, 1)
                pool.iota(iota[:], [[1, W]], base=0, channel_multiplier=0,
                          allow_small_or_imprecise_dtypes=True).then_inc(ident_done, 1)
                pool.wait_ge(ident_done, 2)
                pool.affine_select(out=ident[:], in_=ident[:], compare_op=ALU.not_equal, fill=1.0, base=0,
                                   pattern=[[-1, P]], channel_multiplier=1).then_inc(ident_done, 1)
                pool.memset(acc_b[:], 0.0)
                pool.memset(acc_a[:, 0:2, :], 0.0).then_inc(ident_done, 1)

            @block.tensor
            def _(pe):
                pe.wait_ge(weights_loaded, WEIGHTS)
                pe.matmul(banks[0][0:64, 0:64], w1t, ws, start=True, stop=True)
                pe.matmul(banks[1][:, 0:64], w2t, ws, start=True, stop=True)
                pe.matmul(banks[2][0:64, 0:32], w3t, wv, start=True, stop=True)
                pe.matmul(banks[3][:, 0:32], w4t, wv, start=True, stop=True)
                pe.matmul(banks[4][:, 0:32], w5t, wv, start=True, stop=True).then_inc(products_done, 1)

            @block.vector
            def _(dve):
                dve.memset(lin_w[:], 0.0)
                dve.memset(sum_w[:], 0.0).then_inc(zeroed, 1)
                dve.memset(msg_w[:], 0.0)
                dve.memset(eps[:], EPS).then_inc(setup_step, 1)
                dve.wait_ge(dst_loaded, 16)
                dve.tensor_reduce(bmin, dst_rows.bitcast(I32), AX.X, ALU.min).then_inc(setup_step, 1)
                dve.wait_ge(setup_step, 2)
                dve.tensor_scalar(bmin_i, bmin, float(NPAD - W), None, ALU.min).then_inc(bases_found, 1)
                dve.memset(acc_a[:, 2:4, :], 0.0)
                dve.wait_ge(tables_loaded, TABLES)
                dve.wait_ge(bases_loaded, 32)
                rel_k = rel[:].rearrange("p (b k) -> p b k", k=K)
                dve.tensor_tensor(rel_k, rel_k.bitcast(I32), base_b.rearrange("p (b o) -> p b o", o=1)
                                  .to_broadcast([P, BLOCKS, K]), ALU.subtract).then_inc(setup_step, 1)
                dve.wait_ge(setup_step, 3)
                dve.tensor_reduce(far, rel[:], AX.X, ALU.max).then_inc(far_found, 1)
                dve.wait_ge(products_done, 1)
                g1, g2, g3, g4, g5 = (banks[n] for n in range(5))
                c2, c5 = C0 * INV3 * LIN_S, C1 * INV6 * LIN_V
                c34 = C1 * INV3 * LIN_V
                v0, v1, j = slice(64, 96), slice(96, 128), [slice(32 * q, 32 * q + 32) for q in range(4)]
                s_, hs, hv = slice(0, 64), slice(0, 64), [slice(64 + 32 * i, 96 + 32 * i) for i in range(3)]
                places = [
                    (0, s_, hs, g1, C0 * LIN_S), (0, v0, hv[0], g4, c34), (0, v1, hv[1], g4, c34),
                    (1, s_, hv[0], g3, c34), (1, v0, hs, g2, c2), (1, v1, hv[2], g5, -c5),
                    (2, s_, hv[1], g3, c34), (2, v0, hv[2], g5, c5), (2, v1, hs, g2, c2),
                    (3, s_, hv[2], g3, c34), (3, v0, hv[1], g5, -c5), (3, v1, hv[0], g5, c5),
                    (4, j[0], hv[2], g4, c34), (4, j[1], hv[1], g5, c5), (4, j[2], hv[0], g5, -c5), (4, j[3], hs, g2, c2),
                ]
                for part, rows, cols, g, c in places:
                    dve.tensor_scalar(msg_w[rows, part, cols], g[rows, 0:cols.stop - cols.start], float(c), None, ALU.mult)
                dve.wait_ge(places_loaded, PLACES)
                dve.tensor_scalar(lin_w[0:64], lin_w[0:64], float(LIN_S), None, ALU.mult)
                dve.tensor_scalar(lin_w[64:128], lin_w[64:128], float(LIN_V), None, ALU.mult)
                dve.tensor_scalar(lin_wz[:], lin_wz[:], float(LIN_V), None, ALU.mult)
                dve.tensor_scalar(sum_w[:], sum_w[:], SUM_SCALE, None, ALU.mult).then_inc(setup_step, 1)
                dve.wait_ge(setup_step, 4)
                dve.tensor_scalar(sum_w[96:128, 4, 0:64], sum_w[96:128, 4, 0:64], float(INV3), None, ALU.mult)
                dve.wait_ge(far_loaded, 16)
                dve.tensor_reduce(far_max, far_row, AX.X, ALU.max).then_inc(setup_step, 1)
                dve.wait_ge(setup_step, 5)
                dve.tensor_scalar(flag[:], far_max, float(W), None, ALU.is_ge)

        def load_bases(start, n):
            _, values = nc.values_load_multi_w_load_instructions(
                base_row[0:1, bass.ds(start, n)], engines=[DVE], min_val=0, max_val=NPAD - W,
                skip_runtime_bounds_check_because="the bases are held to 0 .. NPAD - W")
            return values

        def iterations(engine, body):
            body(0, True, False)
            with engine.Fori(1, ITERS - 1) as i:
                body(i, False, False)
            body(ITERS - 1, False, True)

        hot0 = [h.rearrange("p k j n -> p k (j n)") for h in hot]

        def vectors_by_attr(dve, dst, rows_in, t):
            return dve.tensor_tensor(dst[:, :, 0:P].rearrange("p k (j u) -> p k j u", j=4),
                                     rows_in[:, :, P:D].rearrange("p k (o u) -> p k o u", o=1).to_broadcast([P, K, 4, MUL1]),
                                     attr(t, 0, 4), ALU.mult)

        def dot_terms(dve, rows_in, t):
            return dve.tensor_tensor(dot3, rows_in[:, :, MUL0:D].rearrange("p k (i u) -> p k i u", i=3), attr(t, 1, 4), ALU.mult)

        def dot_sums(dve):
            return dve.tensor_reduce(dot, dot3.rearrange("p k i u -> p k u i"), AX.X, ALU.add)

        def weighted_rows(dve, z, w, y0, y):
            dve.tensor_tensor(z[:, :, 0:64], w[:, :, 0:64], y0[:, :, 0:64], ALU.mult)
            dve.tensor_tensor(z[:, :, 64:128], w[:, :, 64:128], y[:, :, 0:64], ALU.mult)
            dve.tensor_tensor(z[:, :, 128:224].rearrange("p k (i u) -> p k i u", i=3),
                              w[:, :, 128:160].rearrange("p k (i u) -> p k i u", i=1).to_broadcast([P, K, 3, MUL1]),
                              y0[:, :, 64:160].rearrange("p k (i u) -> p k i u", i=3), ALU.mult)

        def weighted_dots(dve, z, w):
            return dve.tensor_tensor(z[:, :, 224:256], w[:, :, 160:192], dot, ALU.mult)

        w_of = [psum_all[:, 4 + 2 * s:6 + 2 * s, :].rearrange("p b (h d) -> p (b h) d", h=2)[:, 0:K, :] for s in range(2)]

        def far_edges(name, layer, table):
            windows = NPAD // FW
            far_hot = work[:, K * D:K * D + K * 5 * FW].rearrange("p (k j n) -> p k j n", k=K, j=5)
            assert K * 5 * FW <= 4 * K * D
            lo = 5 * K * D
            nodes = work[:, lo:lo + FW]
            far_dst = work[:, lo + FW:lo + FW + K]
            is_far = work[:, lo + FW + K:lo + FW + 2 * K]
            all_dst = work[:, lo + FW + 2 * K:lo + FW + 3 * K].bitcast(I32)
            lists_loaded, rows_gathered, rad_in, hid_lin, hid_out, w_out, scaled_out, operands, hots, window_summed, window_added, block_done = (
                sem(f"far{name}_{n}") for n in ("lists_loaded", "rows_gathered", "rad_in", "hid_lin", "hid_out", "w_out", "scaled_out",
                                                "operands", "hots", "window_summed", "window_added", "block_done"))
            n_lists = 2 * ITERS
            per_list = U // 2

            def if_far(engine, body):
                value = engine.value_load(flag[0:1, 0:1], min_val=0, max_val=1)
                with engine.If(value):
                    with engine.Fori(0, n_lists) as g:
                        body(g)

            with nc.Block() as block:
                @block.sync
                def _(sp):
                    def body(g):
                        for b in range(per_list):
                            c = g * per_list + b
                            sp.wait_ge(block_done, c)
                            if b == 0:
                                sp.dma_start(idx[0][:], a["src"][bass.ds(g, 1)].rearrange("o p t -> (o p) t")).then_inc(lists_loaded, 16)
                            sp.dma_start(all_dst, a["dst_tiles"][:, bass.ds(c * K, K)]).then_inc(lists_loaded, 16)
                            if layer == 1:
                                sp.dma_start(rad[0], a["radial"][bass.ds(c, 1)].rearrange("o p e -> (o p) e")).then_inc(rad_in, 16)
                            wait_apart(sp, lists_loaded, g * (16 * (per_list + 1)) + 16 * (b + 2))
                    if_far(sp, body)

                @block.gpsimd
                def _(pool):
                    def body(g):
                        for b in range(per_list):
                            pool.wait_ge(block_done, g * per_list + b)
                            wait_apart(pool, lists_loaded, g * (16 * (per_list + 1)) + 16 * (b + 2))
                            for k in range(K):
                                t = b * K + k
                                pool.indirect_dma_start(gat[0][:, k, :], None, table, bass.IndirectOffsetOnAxis(idx[0][:, t:t + 1], 0))\
                                    .then_inc(rows_gathered, 16)
                    if_far(pool, body)

                @block.scalar
                def _(act):
                    def body(g):
                        for b in range(per_list):
                            c = g * per_list + b
                            act.wait_ge(hid_lin, c + 1)
                            act.activation(hid[0], banks[2][0:NR, 0:BE], ACT.Relu, scale=RELU_SCALE).then_inc(hid_out, 1)
                            act.wait_ge(rows_gathered, c * (16 * K) + 16 * K)
                            for k in range(K):
                                ins = act.activation(edge_y[0][:, k, :], gat[0][:, k, :], ACT.Copy, scale=sh[:, bass.ds(c * K + k, 1), 0])
                            ins.then_inc(scaled_out, 1)
                    if layer == 1:
                        if_far(act, body)

                @block.tensor
                def _(pe):
                    def body(g):
                        for b in range(per_list):
                            c = g * per_list + b
                            if layer == 1:
                                pe.wait_ge(rad_in, c * 16 + 16)
                                pe.matmul(banks[2][0:NR, 0:BE], fc1[:], rad[0], start=True, stop=True).then_inc(hid_lin, 1)
                                pe.wait_ge(hid_out, c + 1)
                                for k in range(K):
                                    mm = pe.matmul(w_of[0][:, k, 0:NW], hid[0][:, k * P:k * P + P], fc2[:], start=True, stop=True)
                                mm.then_inc(w_out, 1)
                            with pe.Fori(0, windows) as w:
                                pe.wait_ge(hots, c * windows + w + 1)
                                first, rest = (far_hot[:, :, 0, :], far_hot[:, :, 1 - layer:5 - layer, :])
                                for k in range(K):
                                    lhs = gat[0][:, k, 0:P] if layer == 0 else prod[0][:, k, 0:P]
                                    pe.matmul(banks[0], lhs, rest[:, k], start=(k == 0), stop=(k == K - 1))
                                for k in range(K):
                                    lhs = prod[0][:, k, 0:P] if layer == 0 else prod[0][:, k, P:2 * P]
                                    mm = pe.matmul(banks[1][:, 0:FW], lhs, first[:, k], start=(k == 0), stop=(k == K - 1))
                                mm.then_inc(window_summed, 1)
                    if_far(pe, body)

                @block.vector
                def _(dve):
                    def spread(t, n):
                        return t.rearrange("p k (j n) -> p k j n", j=1).to_broadcast([P, K, n, FW])

                    def body(g):
                        for b in range(per_list):
                            c = g * per_list + b
                            t = c * K
                            dve.wait_ge(rows_gathered, c * (16 * K) + 16 * K)
                            dve.tensor_scalar(is_far, rel[:, bass.ds(t, K)], float(W), None, ALU.is_ge)
                            dve.drain()
                            dve.scalar_tensor_tensor(out=far_dst, in0=all_dst, scalar=1.0, in1=is_far, op0=ALU.add, op1=ALU.mult)
                            if layer == 0:
                                vectors_by_attr(dve, prod[0], gat[0], t)
                            else:
                                dot_terms(dve, gat[0], t)
                                dve.drain()
                                dot_sums(dve)
                                dve.drain()
                                dve.wait_ge(w_out, c + 1)
                                dve.wait_ge(scaled_out, c + 1)
                                weighted_rows(dve, prod[0], w_of[0], edge_y[0], gat[0])
                                weighted_dots(dve, prod[0], w_of[0])
                            dve.drain().then_inc(operands, 1)
                            with dve.Fori(0, windows) as w:
                                dve.wait_ge(operands, c + 1)
                                dve.tensor_tensor(far_hot[:, :, 0, :], nodes.rearrange("p (o n) -> p o n", o=1).to_broadcast([P, K, FW]),
                                                  far_dst.rearrange("p (k o) -> p k o", o=1).to_broadcast([P, K, FW]), ALU.is_equal)
                                dve.drain()
                                lo_j = 0 if layer == 0 else 1
                                for j in range(lo_j, 4):
                                    dve.tensor_tensor(far_hot[:, :, j + 1 - layer, :], far_hot[:, :, 0, :],
                                                      sh[:, bass.ds(t, K), j:j + 1].to_broadcast([P, K, FW]), ALU.mult)
                                dve.tensor_scalar(nodes, nodes, float(FW), None, ALU.add)
                                dve.drain().then_inc(hots, 1)
                                dve.wait_ge(window_summed, c * windows + w + 1)
                                at = bass.ds(w * FW, FW)
                                dve.tensor_tensor(acc_a[:, :, at], acc_a[:, :, at], banks[0].rearrange("p (j n) -> p j n", j=4), ALU.add)
                                dve.tensor_tensor(acc_b[:, at], acc_b[:, at], banks[1][:, 0:FW], ALU.add)
                                dve.drain().then_inc(window_added, 1)
                            dve.tensor_scalar(nodes, nodes, float(-FW * windows), None, ALU.add)
                            dve.drain().then_inc(block_done, 1)
                    value = dve.value_load(flag[0:1, 0:1], min_val=0, max_val=1)
                    with dve.If(value):
                        for n in range(FW // W):
                            dve.tensor_scalar(nodes[:, n * W:n * W + W], iota[:], float(n * W + 1), None, ALU.add)
                        dve.drain()
                        with dve.Fori(0, n_lists) as g:
                            body(g)

        idx_loaded = [sem(f"idx0_loaded{h}") for h in range(2)]
        gathered = [sem(f"gathered0_{s}") for s in range(U)]
        onehot_built, operands_ready, summed, added = (
            sem("onehot0_built"), sem("operands0_ready"), sem("summed0"), sem("added0"))

        def refill_indices(sp, i, h, loaded, landed):
            for s in range(3 * h, 3 * h + 3):
                sp.wait_ge(landed[s], i * (16 * K) + 16 * K)
            sp.dma_start(idx[h][:], a["src"][bass.ds(i * 2 + (2 + h), 1)].rearrange("o p t -> (o p) t")).then_inc(loaded[h], 16)

        def attr(t, lo, hi):
            return sh[:, bass.ds(t, K), lo:hi].rearrange("p k (j o) -> p k j o", o=1).to_broadcast([P, K, hi - lo, W])

        def onehots(dve, dst, t):
            return dve.tensor_tensor(dst[:, :, 0, :], iota[:].rearrange("p (o n) -> p o n", o=1).to_broadcast([P, K, W]),
                                     rel[:, bass.ds(t, K)].rearrange("p (k o) -> p k o", o=1).to_broadcast([P, K, W]), ALU.is_equal)

        passed = sem("passed")

        def wait_apart(engine, semaphore, value):
            engine.wait_ge(semaphore, value)
            if not isinstance(value, int):
                engine.sem_inc(passed, 1)

        def gather_block(pool, i, q, first, table, loaded, landed, freed):
            h = q // 3
            if q % 3 == 0:
                wait_apart(pool, loaded[h], i * 16 + 16)
            if not first:
                wait_apart(pool, freed, i * U + (q + 1 - U))
            for k in range(K):
                t = q % 3 * K + k
                pool.indirect_dma_start(gat[q][:, k, :], None, table, bass.IndirectOffsetOnAxis(idx[h][:, t:t + 1], 0)).then_inc(landed[q], 16)

        def add_sums(dve, base, bank):
            dst = acc_a[:, :, bass.ds(base, W)]
            dve.tensor_tensor(dst, dst, bank[:, 0:4 * W].rearrange("p (j n) -> p j n", j=4), ALU.add)
            dst = acc_b[:, bass.ds(base, W)]
            return dve.tensor_tensor(dst, dst, bank[:, 4 * W:5 * W], ALU.add)

        with nc.Block() as block:
            @block.sync
            def _(sp):
                for h in range(2):
                    sp.dma_start(idx[h][:], a["src"][h]).then_inc(idx_loaded[h], 16)

                def body(i, first, last):
                    if not last:
                        for h in range(2):
                            refill_indices(sp, i, h, idx_loaded, gathered)
                iterations(sp, body)

            @block.gpsimd
            def _(pool):
                def body(i, first, last):
                    for q in range(U):
                        gather_block(pool, i, q, first, a["x"], idx_loaded, gathered, summed)
                iterations(pool, body)

            @block.vector
            def _(dve):
                def add(c, base, bank):
                    dve.wait_ge(summed, c)
                    if not (isinstance(c, int) and c == 1):
                        dve.wait_ge(added, c - 1)
                    add_sums(dve, base, bank).then_inc(added, 1)

                def body(i, first, last):
                    bases = load_bases(0, U - 1) if first else load_bases(i * U - 1, U)
                    for q in range(U):
                        c = i * U + q
                        t = i * (U * K) + q * K
                        s = q % 2
                        if not first or q >= 2:
                            dve.wait_ge(summed, c - 1)
                        onehots(dve, hot[s], t).then_inc(onehot_built, 1)
                        dve.wait_ge(gathered[q], i * (16 * K) + 16 * K)
                        vectors_by_attr(dve, prod[s], gat[q], t)
                        dve.wait_ge(onehot_built, c + 1)
                        dve.tensor_tensor(hot[s][:, :, 1:5, :], hot[s][:, :, 0:1, :].to_broadcast([P, K, 4, W]), attr(t, 0, 4),
                                          ALU.mult).then_inc(operands_ready, 1)
                        if not first or q >= 1:
                            add(c, bases[q - first], banks[1 - s])
                    if last:
                        add(BLOCKS, load_bases(BLOCKS - 1, 1)[0], banks[1])
                iterations(dve, body)

            @block.tensor
            def _(pe):
                def body(i, first, last):
                    for q in range(U):
                        c, s = i * U + q, q % 2
                        pe.wait_ge(operands_ready, c + 1)
                        if not first or q >= 2:
                            pe.wait_ge(added, c - 1)
                        for k in range(K):
                            pe.matmul(banks[s][:, 0:4 * W], gat[q][:, k, 0:P], hot0[s][:, k, W:5 * W],
                                      start=(k == 0), stop=(k == K - 1))
                        for k in range(K):
                            mm = pe.matmul(banks[s][:, 4 * W:5 * W], prod[s][:, k, 0:P], hot0[s][:, k, 0:W],
                                           start=(k == 0), stop=(k == K - 1))
                        mm.then_inc(summed, 1)
                iterations(pe, body)

        far_edges("0", 0, a["x"])

        used[0] = 0
        PAIR = 2
        BATCHES = NT // PAIR
        assert NT % PAIR == 1 and BATCHES % 2 == 0

        def pair_buffers(cols, parts=P, inner=PAIR):
            return [carve(inner * cols, parts).rearrange("p (t d) -> p t d", t=inner) for _ in range(2)]

        x_in, res, nrm, y_out, pre_out = (pair_buffers(D) for _ in range(5))
        trn_a, trn_b = pair_buffers(P), pair_buffers(P, MUL1)
        stage = pair_buffers(PAIR * P, inner=5)
        zeros = carve(PAIR * P)
        stats, mv = pair_buffers(6), pair_buffers(2)
        std, rstd = pair_buffers(1), pair_buffers(1)

        def rows(t, start, n):
            return t.rearrange("(t p) d -> p t d", p=P)[:, bass.ds(start, n), :]

        def batches(engine, body):
            body(0, 0, 0, PAIR)
            body(1, 0, 1, PAIR)
            with engine.Fori(1, BATCHES // 2) as i:
                body(i * 2, i, 0, PAIR)
                body(i * 2 + 1, i, 1, PAIR)
            body(BATCHES, BATCHES // 2, 0, 1)

        def early(m, n):
            return isinstance(m, int) and m < n

        def stage_sums(pool, m, s, n, staged, used_up):
            if not early(m, 2):
                wait_apart(pool, used_up, m - 1)
            at = bass.ds(m * (PAIR * P), n * P)
            pool.tensor_copy(stage[s][:, 0:4, 0:n * P], acc_a[:, :, at])
            return at, pool.tensor_copy(stage[s][:, 4, 0:n * P], acc_b[:, at]).then_inc(staged, 1)

        def layer_norm(dve, m, s, n, res_done, stats_done, var_done, std_done, rstd_done):
            dve.wait_ge(res_done, m + 1)
            for t in range(n):
                ins = dve.bn_stats(stats[s][:, t, :], res[s][:, t, :])
            ins.then_inc(stats_done, 1)
            wait_apart(dve, stats_done, m + 1)
            for t in range(n):
                ins = dve.bn_aggr(mv[s][:, t, :], stats[s][:, t, :])
            ins.then_inc(var_done, 1)
            dve.wait_ge(std_done, m + 1)
            dve.reciprocal(rstd[s][:, 0:n, :], std[s][:, 0:n, :]).then_inc(rstd_done, 1)
            dve.wait_ge(rstd_done, m + 1)

        x_loaded, y_stored, pre_stored = ([sem(f"mid_{n}{s}") for s in range(2)] for n in ("x_loaded", "y_stored", "pre_stored"))
        (zeros_done, staged, hidden_done, res_half, res_done, stats_done, var_done, std_done, rstd_done, norm_done, transposed,
         trn_copied, lin_done, y_copied, pre_done) = (sem("mid_" + n) for n in (
             "zeros_done", "staged", "hidden_done", "res_half", "res_done", "stats_done", "var_done", "std_done", "rstd_done",
             "norm_done", "transposed", "trn_copied", "lin_done", "y_copied", "pre_done"))

        with nc.Block() as block:
            @block.sync
            def _(sp):
                def store(m, s, n):
                    sp.wait_ge(y_copied, m + 1)
                    sp.dma_start(rows(y_dram, m * PAIR, n), y_out[s][:, 0:n, :]).then_inc(y_stored[s], 16)
                    sp.wait_ge(pre_done, m + 1)
                    sp.dma_start(rows(pre_dram, m * PAIR, n), pre_out[s][:, 0:n, :]).then_inc(pre_stored[s], 16)

                def body(m, i, s, n):
                    if not early(m, 2):
                        sp.wait_ge(res_done, m - 1)
                    sp.dma_start(x_in[s][:, 0:n, :], rows(a["x"], m * PAIR, n)).then_inc(x_loaded[s], 16)
                    if not early(m, 2):
                        store(m - 2, s, PAIR)

                batches(sp, body)
                store(BATCHES - 1, 1, PAIR)
                store(BATCHES, 0, 1)
                for s in range(2):
                    sp.wait_ge(y_stored[s], 16 * (BATCHES // 2 + 1 - s))
                    sp.wait_ge(pre_stored[s], 16 * (BATCHES // 2 + 1 - s))

            @block.gpsimd
            def _(pool):
                pool.memset(zeros, 0.0).then_inc(zeros_done, 1)
                pool.wait_ge(zeros_done, 1)

                def body(m, i, s, n):
                    at, _ = stage_sums(pool, m, s, n, staged, hidden_done)
                    wait_apart(pool, staged, m + 1)
                    for part in range(4):
                        pool.tensor_copy(acc_a[:, part, at], zeros[:, 0:n * P])
                    pool.tensor_copy(acc_b[:, at], zeros[:, 0:n * P])
                batches(pool, body)

            @block.tensor
            def _(pe):
                def hidden(m, s, n):
                    pe.wait_ge(staged, m + 1)
                    if not early(m, 2):
                        pe.wait_ge(res_half, m - 1)
                    for t in range(n):
                        for part in range(5):
                            mm = pe.matmul(banks[s][:, t * D:t * D + D], stage[s][:, part, t * P:t * P + P], msg_w[:, part, :],
                                           start=(part == 0), stop=(part == 4))
                    mm.then_inc(hidden_done, 1)

                def linear(m, s, n):
                    pe.wait_ge(norm_done, m + 1)
                    if not early(m, 2):
                        pe.wait_ge(trn_copied, m - 1)
                    for t in range(n):
                        pe.transpose(banks[2 + s][:, t * P:t * P + P], nrm[s][:, t, 0:P], ident[:])
                        lo = PAIR * P + t * P
                        mm = pe.transpose(banks[2 + s][0:MUL1, lo:lo + P], nrm[s][:, t, P:D], ident[:])
                    mm.then_inc(transposed, 1)
                    pe.wait_ge(trn_copied, m + 1)
                    if not early(m, 2):
                        pe.wait_ge(pre_done, m - 1)
                    for t in range(n):
                        dst = banks[4 + 2 * s + t][:, 0:2 * D].rearrange("p (l d) -> p l d", l=2)
                        pe.matmul(dst[:, :, 0:P], trn_a[s][:, t, :], lin_w[:], start=True, stop=True)
                        mm = pe.matmul(dst[:, :, P:D], trn_b[s][:, t, :], lin_wz[:], start=True, stop=True)
                    mm.then_inc(lin_done, 1)

                def body(m, i, s, n):
                    hidden(m, s, n)
                    if not early(m, 1):
                        linear(m - 1, 1 - s, PAIR)
                batches(pe, body)
                linear(BATCHES, 0, 1)

            @block.vector
            def _(dve):
                def outputs(m, before, s, n):
                    dve.wait_ge(y_copied, m + 1)
                    if not early(m, 2):
                        dve.wait_ge(pre_stored[s], before * 16)
                    for t in range(n):
                        ins = dve.scalar_tensor_tensor(out=pre_out[s][:, t, :], in0=banks[4 + 2 * s + t][:, D:2 * D],
                                                       scalar=node_attr[:, bass.ds(m * PAIR + t, 1)],
                                                       in1=nrm[s][:, t, :], op0=ALU.mult, op1=ALU.add)
                    ins.then_inc(pre_done, 1)

                def body(m, i, s, n):
                    dve.wait_ge(hidden_done, m + 1)
                    dve.wait_ge(x_loaded[s], i * 16 + 16)
                    if not early(m, 2):
                        dve.wait_ge(norm_done, m - 1)
                    for t in range(n):
                        ins = dve.scalar_tensor_tensor(out=res[s][:, t, :], in0=banks[s][:, t * D:t * D + D], scalar=0.0,
                                                       in1=x_in[s][:, t, :], op0=ALU.max, op1=ALU.add)
                    ins.then_inc(res_half, 1)
                    dve.wait_ge(res_half, m + 1)
                    dve.tensor_tensor(res[s][:, 0:n, :], res[s][:, 0:n, :], x_in[s][:, 0:n, :], ALU.add).then_inc(res_done, 1)
                    layer_norm(dve, m, s, n, res_done, stats_done, var_done, std_done, rstd_done)
                    if not early(m, 2):
                        dve.wait_ge(transposed, m - 1)
                        dve.wait_ge(pre_done, m - 1)
                    for t in range(n):
                        ins = dve.tensor_scalar(nrm[s][:, t, :], res[s][:, t, :], mv[s][:, t, 0:1], rstd[s][:, t, 0:1],
                                                ALU.subtract, ALU.mult)
                    ins.then_inc(norm_done, 1)
                    if not early(m, 1):
                        outputs(m - 1, i - 1 + s, 1 - s, PAIR)
                batches(dve, body)
                outputs(BATCHES, BATCHES // 2, 0, 1)

            @block.scalar
            def _(act):
                act.preload_act_table(ACT.Sqrt)

                def copies(m, before, s, n):
                    act.wait_ge(transposed, m + 1)
                    if not early(m, 2):
                        act.wait_ge(lin_done, m - 1)
                    act.activation(trn_a[s][:, 0:n, :], banks[2 + s][:, 0:n * P].rearrange("p (t n) -> p t n", t=n), ACT.Copy)
                    lo = PAIR * P
                    act.activation(trn_b[s][:, 0:n, :], banks[2 + s][0:MUL1, lo:lo + n * P].rearrange("p (t n) -> p t n", t=n),
                                   ACT.Copy).then_inc(trn_copied, 1)
                    act.wait_ge(lin_done, m + 1)
                    if not early(m, 2):
                        act.wait_ge(y_stored[s], before * 16)
                    for t in range(n):
                        ins = act.activation(y_out[s][:, t, :], banks[4 + 2 * s + t][:, 0:D], ACT.Copy,
                                             scale=node_attr[:, bass.ds(m * PAIR + t, 1)])
                    ins.then_inc(y_copied, 1)

                def body(m, i, s, n):
                    act.wait_ge(var_done, m + 1)
                    act.activation(std[s][:, 0:n, :], mv[s][:, 0:n, 1:2], ACT.Sqrt, bias=eps[:]).then_inc(std_done, 1)
                    if not early(m, 1):
                        copies(m - 1, i - 1 + s, 1 - s, PAIR)
                batches(act, body)
                copies(BATCHES, BATCHES // 2, 0, 1)

        idx_loaded1 = [sem(f"idx1_loaded{h}") for h in range(2)]
        gathered1 = [sem(f"gathered1_{s}") for s in range(U)]
        rad_loaded = [sem(f"rad_loaded{s}") for s in range(U)]
        onehot_built1, dot3_built, dot_built, scaled, hid_lin_done, hid_done, w_done, z_ready, summed1, added1 = (
            sem(n) for n in ("onehot1_built", "dot3_built", "dot_built", "scaled", "hid_lin_done", "hid_done", "w_done", "z_ready",
                             "summed1", "added1"))
        with nc.Block() as block:
            @block.sync
            def _(sp):
                for h in range(2):
                    sp.dma_start(idx[h][:], a["src"][h]).then_inc(idx_loaded1[h], 16)
                for q in range(U):
                    sp.dma_start(rad[q], a["radial"][q]).then_inc(rad_loaded[q], 16)

                def body(i, first, last):
                    for q in range(U):
                        if not (first and q < 3) and not (last and q >= 3):
                            sp.wait_ge(hid_lin_done, i * U + (q - 2))
                            sp.dma_start(rad[(q + 3) % U], a["radial"][bass.ds(i * U + (q + 3), 1)].rearrange("o p e -> (o p) e"))\
                              .then_inc(rad_loaded[(q + 3) % U], 16)
                        if q % 3 == 2 and not last:
                            refill_indices(sp, i, q // 3, idx_loaded1, gathered1)
                iterations(sp, body)

            @block.gpsimd
            def _(pool):
                def body(i, first, last):
                    for q in range(U):
                        gather_block(pool, i, q, first, y_dram, idx_loaded1, gathered1, summed1)
                iterations(pool, body)

            @block.tensor
            def _(pe):
                def hidden(c, q, uses):
                    pe.wait_ge(rad_loaded[q], uses * 16)
                    if not early(c, 2):
                        pe.wait_ge(hid_done, c - 1)
                    pe.matmul(banks[2 + q % 2][0:NR, 0:BE], fc1[:], rad[q], start=True, stop=True).then_inc(hid_lin_done, 1)

                def sums(c, s):
                    pe.wait_ge(z_ready, c + 1)
                    if not early(c, 2):
                        pe.wait_ge(added1, c - 1)
                    for k in range(K):
                        pe.matmul(banks[s][:, 0:4 * W], prod[s][:, k, 0:P], hot0[s][:, k, 0:4 * W], start=(k == 0), stop=(k == K - 1))
                    for k in range(K):
                        mm = pe.matmul(banks[s][:, 4 * W:5 * W], prod[s][:, k, P:2 * P], hot0[s][:, k, 0:W],
                                       start=(k == 0), stop=(k == K - 1))
                    mm.then_inc(summed1, 1)

                hidden(0, 0, 1)

                def body(i, first, last):
                    for q in range(U):
                        c, s = i * U + q, q % 2
                        if not (last and q == U - 1):
                            hidden(c + 1, (q + 1) % U, i + 1 + (q + 1) // U)
                        pe.wait_ge(hid_done, c + 1)
                        if not early(c, 2):
                            pe.wait_ge(z_ready, c - 1)
                        for k in range(K):
                            mm = pe.matmul(w_of[s][:, k, 0:NW], hid[s][:, k * P:k * P + P], fc2[:], start=True, stop=True)
                        mm.then_inc(w_done, 1)
                        if not early(c, 1):
                            sums(c - 1, 1 - s)
                iterations(pe, body)
                sums(BLOCKS - 1, 1)

            @block.scalar
            def _(act):
                act.preload_act_table(ACT.Relu)

                def relu(c, s):
                    act.wait_ge(hid_lin_done, c + 1)
                    if not early(c, 2):
                        act.wait_ge(w_done, c - 1)
                    act.activation(hid[s], banks[2 + s][0:NR, 0:BE], ACT.Relu, scale=RELU_SCALE).then_inc(hid_done, 1)

                relu(0, 0)

                def body(i, first, last):
                    for q in range(U):
                        c, s = i * U + q, q % 2
                        if not (last and q == U - 1):
                            relu(c + 1, 1 - s)
                        act.wait_ge(gathered1[q], i * (16 * K) + 16 * K)
                        if not early(c, 2):
                            act.wait_ge(z_ready, c - 1)
                        for k in range(K):
                            ins = act.activation(edge_y[s][:, k, :], gat[q][:, k, :], ACT.Copy,
                                                 scale=sh[:, bass.ds(i * (U * K) + (q * K + k), 1), 0])
                        ins.then_inc(scaled, 1)
                iterations(act, body)

            @block.vector
            def _(dve):
                def add(c, base, bank):
                    dve.wait_ge(summed1, c)
                    if not early(c, 2):
                        dve.wait_ge(added1, c - 1)
                    add_sums(dve, base, bank).then_inc(added1, 1)

                def body(i, first, last):
                    bases = load_bases(0, U - 1) if first else load_bases(i * U - 1, U)
                    for q in range(U):
                        c, s = i * U + q, q % 2
                        t = i * (U * K) + q * K
                        if not early(c, 2):
                            dve.wait_ge(summed1, c - 1)
                        onehots(dve, hot[s], t).then_inc(onehot_built1, 1)
                        dve.wait_ge(gathered1[q], i * (16 * K) + 16 * K)
                        if not early(c, 1):
                            dve.wait_ge(dot_built, c)
                        dot_terms(dve, gat[q], t).then_inc(dot3_built, 1)
                        dve.wait_ge(onehot_built1, c + 1)
                        dve.tensor_tensor(hot[s][:, :, 1:4, :], hot[s][:, :, 0:1, :].to_broadcast([P, K, 3, W]), attr(t, 1, 4), ALU.mult)
                        dve.wait_ge(dot3_built, c + 1)
                        if not early(c, 1):
                            dve.wait_ge(z_ready, c)
                        dot_sums(dve).then_inc(dot_built, 1)
                        dve.wait_ge(w_done, c + 1)
                        dve.wait_ge(scaled, c + 1)
                        weighted_rows(dve, prod[s], w_of[s], edge_y[s], gat[q])
                        dve.wait_ge(dot_built, c + 1)
                        weighted_dots(dve, prod[s], w_of[s]).then_inc(z_ready, 1)
                        if not early(c, 1):
                            add(c, bases[q - first], banks[1 - s])
                    if last:
                        add(BLOCKS, load_bases(BLOCKS - 1, 1)[0], banks[1])
                iterations(dve, body)

        far_edges("1", 1, y_dram)

        pre_loaded, out_stored = ([sem(f"end_{n}{s}") for s in range(2)] for n in ("pre_loaded", "out_stored"))
        e_staged, e_sums_done, e_res_done, e_stats_done, e_var_done, e_std_done, e_rstd_done, e_norm_done = (
            sem("end_" + n) for n in ("staged", "sums_done", "res_done", "stats_done", "var_done", "std_done", "rstd_done", "norm_done"))

        with nc.Block() as block:
            @block.sync
            def _(sp):
                def store(m, s):
                    sp.wait_ge(e_norm_done, m + 1)
                    sp.dma_start(out[bass.ds(m * (PAIR * P), PAIR * P), :].rearrange("(t p) d -> p t d", p=P), nrm[s]).then_inc(out_stored[s], 16)

                def body(m, i, s, n):
                    if not early(m, 2):
                        sp.wait_ge(e_res_done, m - 1)
                    sp.dma_start(x_in[s][:, 0:n, :], rows(pre_dram, m * PAIR, n)).then_inc(pre_loaded[s], 16)
                    if not early(m, 2):
                        store(m - 2, s)

                batches(sp, body)
                store(BATCHES - 1, 1)
                sp.wait_ge(e_norm_done, BATCHES + 1)
                left = N - (NT - 1) * P
                sp.dma_start(out[N - left:N, :], nrm[0][0:left, 0, :]).then_inc(out_stored[0], 16)
                for s in range(2):
                    sp.wait_ge(out_stored[s], 16 * (BATCHES // 2 + 1 - s))

            @block.gpsimd
            def _(pool):
                batches(pool, lambda m, i, s, n: stage_sums(pool, m, s, n, e_staged, e_sums_done))

            @block.tensor
            def _(pe):
                def body(m, i, s, n):
                    pe.wait_ge(e_staged, m + 1)
                    if not early(m, 2):
                        pe.wait_ge(e_res_done, m - 1)
                    for t in range(n):
                        dst, at = banks[s][:, t * D:t * D + D], slice(t * P, t * P + P)
                        for part in range(5):
                            mm = pe.matmul(dst, stage[s][:, part, at], sum_w[:, part, :], start=(part == 0), stop=(part == 4))
                    mm.then_inc(e_sums_done, 1)
                batches(pe, body)

            @block.vector
            def _(dve):
                def body(m, i, s, n):
                    dve.wait_ge(e_sums_done, m + 1)
                    dve.wait_ge(pre_loaded[s], i * 16 + 16)
                    if not early(m, 2):
                        dve.wait_ge(e_norm_done, m - 1)
                    for t in range(n):
                        ins = dve.scalar_tensor_tensor(out=res[s][:, t, :], in0=banks[s][:, t * D:t * D + D],
                                                       scalar=node_attr[:, bass.ds(m * PAIR + t, 1)], in1=x_in[s][:, t, :],
                                                       op0=ALU.mult, op1=ALU.add)
                    ins.then_inc(e_res_done, 1)
                    layer_norm(dve, m, s, n, e_res_done, e_stats_done, e_var_done, e_std_done, e_rstd_done)
                    if not early(m, 2):
                        dve.wait_ge(out_stored[s], i * 16)
                    for t in range(n):
                        ins = dve.tensor_scalar(nrm[s][:, t, :], res[s][:, t, :], mv[s][:, t, 0:1], rstd[s][:, t, 0:1],
                                                ALU.subtract, ALU.mult)
                    ins.then_inc(e_norm_done, 1)
                batches(dve, body)

            @block.scalar
            def _(act):
                act.preload_act_table(ACT.Sqrt)

                def body(m, i, s, n):
                    act.wait_ge(e_var_done, m + 1)
                    act.activation(std[s][:, 0:n, :], mv[s][:, 0:n, 1:2], ACT.Sqrt, bias=eps[:]).then_inc(e_std_done, 1)
                batches(act, body)


def kernel(**inputs):
    import concourse.bacc as _bacc
    from concourse.bass_utils import run_bass_kernel_spmd as _run

    arr = {k: np.asarray(v) for k, v in inputs.items()}
    order = np.concatenate([np.arange(MUL0), (MUL0 + 3 * np.arange(MUL1)[None, :] + np.arange(3)[:, None]).reshape(-1)])
    back = np.argsort(order)

    def edges(v, fill=0):
        return np.concatenate([v, np.full((EPAD - E,) + v.shape[1:], fill, v.dtype)])

    def by_tile(v):
        return np.ascontiguousarray(v.reshape((TILES, P) + v.shape[1:]).swapaxes(0, 1))

    dst, src = edges(arr["dst"], N - 1), edges(arr["src"])
    nodes = {"x": arr["x"][:, order], "node_attr": arr["node_vec1"]}
    nodes = {k: np.concatenate([v, np.zeros((NPAD - N,) + v.shape[1:], v.dtype)]) for k, v in nodes.items()}
    arrays = {
        "x": nodes["x"],
        "node_attr": nodes["node_attr"].reshape(NT, P).T,
        "dst": dst, "dst_tiles": by_tile(dst),
        "src": src.reshape(2 * ITERS, H, P).swapaxes(1, 2),
        "sh": by_tile(edges(arr["edge_attr_4"])),
        "radial": edges(arr["edge_attr_10"]).reshape(BLOCKS, BE, NB).swapaxes(1, 2),
        "W1t": arr["L0_gnn_W1"].T, "W2t": arr["L0_gnn_W2"].T, "W3t": arr["L0_gnn_W3"].T,
        "W4t": arr["L0_gnn_W4"].T, "W5t": arr["L0_gnn_W5"].T, "Ws": arr["L0_gnn_Ws"], "Wv": arr["L0_gnn_Wv"],
        "fc1": arr["L1_gnn_W_fc1"], "fc2": arr["L1_gnn_W_fc2"],
    }
    for k in ("W_si0", "W_si1", "W_l1_0", "W_l1_1", "W_l2_00", "W_l2_10", "W_l2_01", "W_l2_11"):
        arrays[k] = arr["L1_gnn_" + k]
    arrays = {k: np.ascontiguousarray(v) for k, v in arrays.items()}
    nc = _bacc.Bacc("TRN2", target_bir_lowering=False, num_devices=1)
    args = {k: nc.dram_tensor("in_" + k, v.shape, mybir.dt.from_np(v.dtype), kind="ExternalInput").ap() for k, v in arrays.items()}
    out = nc.dram_tensor("out_rows", (N, D), F32, kind="ExternalOutput").ap()
    build(nc, args, out)
    r = _run(nc, [{"in_" + k: v for k, v in arrays.items()}], core_ids=[0])
    return r.results[0]["out_rows"][:, back]
```

```python
from contextlib import ExitStack

import numpy as np

import concourse.bass as bass
from concourse import mybir

F32 = mybir.dt.float32
I32 = mybir.dt.int32
ALU = mybir.AluOpType
ACT = mybir.ActivationFunctionType
AX = mybir.AxisListType
DVE = mybir.EngineType.DVE

P = 128
N, E = 6250, 200000
MUL0, MUL1 = 64, 32
D = MUL0 + 3 * MUL1
NB, NR = 10, 100
NW = 2 * MUL0 + 2 * MUL1
NT = -(-N // P)
NPAD = NT * P
K = 3
BE = K * P
W = 32
U = 6
H = U // 2 * K
ITERS = -(-E // (BE * U))
BLOCKS = ITERS * U
TILES = BLOCKS * K
EPAD = TILES * P
FW = P
EARLY = 41
NE = ITERS - EARLY

EPS = 1e-5
C0 = 1.0 / np.sqrt(MUL0 + MUL1)
C1 = np.sqrt(3.0 / (MUL0 + 2 * MUL1))
INV3, INV6 = 1.0 / np.sqrt(3.0), 1.0 / np.sqrt(6.0)
LIN_S, LIN_V = 1.0 / np.sqrt(MUL0), 1.0 / np.sqrt(MUL1)
RELU_SCALE = float(np.sqrt(2.0) / np.sqrt(NB))
SUM_SCALE = float(0.5 / np.sqrt(MUL0 + MUL1) / np.sqrt(16.0) / np.sqrt(NR))


def build(nc, a, out):
    with ExitStack() as ctx:
        def sb(name, shape, dt=F32):
            return ctx.enter_context(nc.sbuf_tensor(name, shape, dt))

        def sem(name):
            return ctx.enter_context(nc.semaphore(name))

        def dram(name, shape, dt=F32):
            return nc.dram_tensor(name, shape, dt).ap()

        acc_a = sb("acc_a", [P, 4, NPAD])
        acc_b = sb("acc_b", [P, NPAD])
        sh = sb("sh", [P, TILES, 4])
        rel = sb("rel", [P, TILES])
        iota = sb("iota", [P, W])
        ident = sb("ident", [P, P])
        base_row = sb("base_row", [1, BLOCKS], I32)
        flags = sb("flags", [1, 3], I32)
        node_attr = sb("node_attr", [P, NT])
        msg_w = sb("msg_w", [P, 5, D])
        lin_w = sb("lin_w", [P, 2, P])
        lin_wz = sb("lin_wz", [MUL1, 2, MUL1])
        sum_w = sb("sum_w", [P, 3, D])
        fc1 = sb("fc1", [NB, NR])
        fc2 = sb("fc2", [NR, NW])
        idx = [sb(f"idx{h}", [P, H], I32) for h in range(2)]
        eps = sb("eps", [P, 1])
        zeros = sb("zeros", [P, P])

        ROOM = 10880 + 320
        work = sb("work", [P, ROOM])
        used = [0]

        def carve(cols, parts=P):
            lo = used[0]
            used[0] += cols
            assert used[0] <= ROOM
            return work[0:parts, lo:lo + cols]

        def thirds(cols, k=K):
            return carve(k * cols).rearrange("p (k d) -> p k d", k=k)

        gat = [thirds(D) for _ in range(U)]
        hot = [carve(K * 5 * W).rearrange("p (k j n) -> p k j n", k=K, j=5) for _ in range(2)]
        prod = [thirds(256) for _ in range(2)]
        stage = carve(5 * P).rearrange("p (a n) -> p a n", a=5)
        x_in, res, nrm = carve(D), carve(D), carve(D)
        stats, mv, std, rstd = carve(6), carve(2), carve(1), carve(1)
        edge_y0 = used[0]
        edge_y = [thirds(D) for _ in range(2)]
        dot3 = carve(K * 96).rearrange("p (k i u) -> p k i u", k=K, i=3)
        hid = [carve(BE, NR) for _ in range(2)]
        rad = [carve(BE, NB) for _ in range(U)]
        used[0] = edge_y0
        trn_a, trn_b = carve(P), carve(P, MUL1)
        y_bufs, pre_bufs = ([carve(D) for _ in range(1 + NT - NE)] for _ in range(2))
        x_last = [[carve(D) for _ in range(NT - NE)], [edge_y[1][:, k, :] for k in range(NT - NE)]]
        assert NT - NE <= K

        psum_all = ctx.enter_context(nc.psum_tensor("psum_all", [P, 8, 512], F32))
        banks = [psum_all[:, n, :] for n in range(8)]
        w_of = [psum_all[:, 4 + 2 * s:6 + 2 * s, :].rearrange("p b (h d) -> p (b h) d", h=2)[:, 0:K, :] for s in range(2)]

        base_dram = dram("base_dram", [BLOCKS], I32)
        measures_dram = dram("measures_dram", [2, P])
        y_dram = dram("y_dram", [NPAD, D])
        pre_dram = dram("pre_dram", [NPAD, D])
        passed = sem("passed")

        def early(m, n):
            return isinstance(m, int) and m < n

        def wait_apart(engine, semaphore, value):
            engine.wait_ge(semaphore, value)
            if not isinstance(value, int):
                engine.sem_inc(passed, 1)

        def load_bases(start, n):
            _, values = nc.values_load_multi_w_load_instructions(
                base_row[0:1, bass.ds(start, n)], engines=[DVE], min_val=0, max_val=NPAD - W,
                skip_runtime_bounds_check_because="the bases are held to 0 .. NPAD - W")
            return values

        def load_flags(engine):
            engine.wait_ge(flags_set, 1)
            return [engine.value_load(flags[0:1, n:n + 1], min_val=0, max_val=1) for n in range(3)]

        def iterations(engine, body, found=None):
            body(0, True, False, None)
            with engine.Fori(1, EARLY) as i:
                body(i, False, False, None)
            found = found or load_flags(engine)
            _, late, in_order = found
            with engine.If(in_order):
                body(EARLY, False, False, 0)
                with engine.Fori(EARLY + 1, ITERS - 1) as i:
                    body(i, False, False, i - EARLY)
                body(ITERS - 1, False, True, NE - 1)
            with engine.If(late):
                with engine.Fori(EARLY, ITERS - 1) as i:
                    body(i, False, False, None)
                body(ITERS - 1, False, True, None)
            return found

        def refill_indices(sp, i, h, loaded, landed):
            for s in range(3 * h, 3 * h + 3):
                sp.wait_ge(landed[s], i * (16 * K) + 16 * K)
            sp.dma_start(idx[h][:], a["src"][bass.ds(i * 2 + (2 + h), 1)].rearrange("o p t -> (o p) t")).then_inc(loaded[h], 16)

        def gather_block(pool, i, q, first, table, loaded, landed, freed):
            h = q // 3
            if q % 3 == 0:
                wait_apart(pool, loaded[h], i * 16 + 16)
            if not first:
                wait_apart(pool, freed, i * U + (q + 1 - U))
            for k in range(K):
                t = q % 3 * K + k
                pool.indirect_dma_start(gat[q][:, k, :], None, table, bass.IndirectOffsetOnAxis(idx[h][:, t:t + 1], 0)).then_inc(landed[q], 16)

        def attr(t, lo, hi):
            return sh[:, bass.ds(t, K), lo:hi].rearrange("p k (j o) -> p k j o", o=1).to_broadcast([P, K, hi - lo, W])

        def onehots(dve, dst, t):
            return dve.tensor_tensor(dst[:, :, 0, :], iota[:].rearrange("p (o n) -> p o n", o=1).to_broadcast([P, K, W]),
                                     rel[:, bass.ds(t, K)].rearrange("p (k o) -> p k o", o=1).to_broadcast([P, K, W]), ALU.is_equal)

        def dot_terms(dve, rows_in, t):
            return dve.tensor_tensor(dot3, rows_in[:, :, MUL0:D].rearrange("p k (i u) -> p k i u", i=3), attr(t, 1, 4), ALU.mult)

        def dot_sums(dve, z):
            return dve.tensor_reduce(z[:, :, 224:256], dot3.rearrange("p k i u -> p k u i"), AX.X, ALU.add)

        def weighted_rows(dve, z, w, y0, y):
            dve.tensor_tensor(z[:, :, 0:64], w[:, :, 0:64], y0[:, :, 0:64], ALU.mult)
            dve.tensor_tensor(z[:, :, 64:128], w[:, :, 64:128], y[:, :, 0:64], ALU.mult)
            dve.tensor_tensor(z[:, :, 128:224].rearrange("p k (i u) -> p k i u", i=3),
                              w[:, :, 128:160].rearrange("p k (i u) -> p k i u", i=1).to_broadcast([P, K, 3, MUL1]),
                              y0[:, :, 64:160].rearrange("p k (i u) -> p k i u", i=3), ALU.mult)

        def weighted_dots(dve, z, w):
            return dve.tensor_tensor(z[:, :, 224:256], w[:, :, 160:192], z[:, :, 224:256], ALU.mult)

        def block_sums(pe, layer, bank, rows, hots):
            for k in range(K):
                pe.matmul(bank[0].rearrange("p (j n) -> p j n", j=4), rows[:, k, 0:P], hots[:, k, 1 - layer:5 - layer, :],
                          start=(k == 0), stop=(k == K - 1))
            for j in range(4 if layer == 0 else 1):
                for k in range(K):
                    if layer == 0:
                        mm = pe.matmul(bank[1][32 * j:32 * j + 32, :], rows[:, k, P:D], hots[:, k, 1 + j, :], start=(k == 0), stop=(k == K - 1))
                    else:
                        mm = pe.matmul(bank[1], rows[:, k, P:2 * P], hots[:, k, 0, :], start=(k == 0), stop=(k == K - 1))
            return mm

        def sum_bank(s):
            return banks[s][:, 0:4 * W], banks[s][:, 4 * W:5 * W]

        def add_sums(dve, c, bank, base, summed, added):
            dve.wait_ge(summed, c)
            if not early(c, 2):
                dve.wait_ge(added, c - 1)
            dst = acc_a[:, :, bass.ds(base, W)]
            dve.tensor_tensor(dst, dst, bank[:, 0:4 * W].rearrange("p (j n) -> p j n", j=4), ALU.add)
            dst = acc_b[:, bass.ds(base, W)]
            dve.tensor_tensor(dst, dst, bank[:, 4 * W:5 * W], ALU.add).then_inc(added, 1)

        def tile_rows(t, n):
            return t[bass.ds(n * P, P), :]

        class Node:

            def __init__(self, name, layer):
                self.layer = layer
                (self.staged, self.summed, self.half, self.res_done, self.stats_done, self.var_done, self.std_done, self.rstd_done,
                 self.norm_done, self.x_loaded, self.rows_stored) = (sem(f"{name}_{n}") for n in (
                     "staged", "summed", "half", "res_done", "stats_done", "var_done", "std_done", "rstd_done", "norm_done",
                     "x_loaded", "rows_stored"))
                if layer == 0:
                    self.transposed, self.trn_copied, self.lin_done, self.y_copied, self.pre_done, self.y_stored = (
                        sem(f"{name}_{n}") for n in ("transposed", "trn_copied", "lin_done", "y_copied", "pre_done", "y_stored"))

            def rows_out(self, last):
                return nrm if self.layer == 0 or last is None else edge_y[0][:, last, :]

            def load(self, sp, t, table):
                if not early(t, 1):
                    sp.wait_ge(self.res_done if self.layer == 0 else self.half, t)
                sp.dma_start(x_in, tile_rows(table, t)).then_inc(self.x_loaded, 16)

            def store(self, sp, t, last=None):
                if self.layer == 0:
                    n = 0 if last is None else 1 + last
                    sp.wait_ge(self.y_copied, t + 1)
                    sp.dma_start(tile_rows(y_dram, t), y_bufs[n]).then_inc(self.y_stored, 16)
                    sp.wait_ge(self.pre_done, t + 1)
                    sp.dma_start(tile_rows(pre_dram, t), pre_bufs[n]).then_inc(self.rows_stored, 16)
                    return
                sp.wait_ge(self.norm_done, t + 1)
                if isinstance(t, int) and t == NT - 1:
                    left = N - (NT - 1) * P
                    sp.dma_start(out[N - left:N, :], self.rows_out(last)[0:left, :]).then_inc(self.rows_stored, 16)
                else:
                    sp.dma_start(tile_rows(out, t), self.rows_out(last)).then_inc(self.rows_stored, 16)

            def stage_sums(self, act, t, added=None):
                if added is not None:
                    act.wait_ge(*added)
                if not early(t, 1):
                    act.wait_ge(self.summed, t)
                at = bass.ds(t * P, P)
                if self.layer == 0:
                    act.activation(stage[:, 0:4, :], acc_a[:, :, at], ACT.Copy)
                else:
                    for rows, part, of, n in ((slice(0, 64), 0, slice(0, 64), 0), (slice(64, 128), 0, slice(64, 128), 1),
                                              (slice(0, 64), 1, slice(64, 128), 2), (slice(64, 128), 1, slice(64, 128), 3)):
                        act.activation(stage[rows, part, :], acc_a[of, n, at], ACT.Copy)
                act.activation(stage[:, (4, 2)[self.layer], :], acc_b[:, at], ACT.Copy).then_inc(self.staged, 1)

            def root(self, act, t):
                act.wait_ge(self.var_done, t + 1)
                act.activation(std, mv[:, 1:2], ACT.Sqrt, bias=eps[:]).then_inc(self.std_done, 1)

            def copy_transposed(self, act, t):
                act.wait_ge(self.transposed, t + 1)
                if not early(t, 1):
                    act.wait_ge(self.lin_done, t)
                act.activation(trn_a, banks[3][:, 0:P], ACT.Copy)
                act.activation(trn_b, banks[3][0:MUL1, P:2 * P], ACT.Copy).then_inc(self.trn_copied, 1)

            def copy_y(self, act, t, last=None):
                act.wait_ge(self.lin_done, t + 1)
                if not early(t, 1) and last is None:
                    act.wait_ge(self.y_stored, t * 16)
                act.activation(y_bufs[0 if last is None else 1 + last], banks[4][:, 0:D], ACT.Copy,
                               scale=node_attr[:, bass.ds(t, 1)]).then_inc(self.y_copied, 1)

            def sums(self, pe, t):
                pe.wait_ge(self.staged, t + 1)
                if not early(t, 1):
                    pe.wait_ge(self.half, t)
                w, parts = ((msg_w, 5), (sum_w, 3))[self.layer]
                for n in range(parts):
                    mm = pe.matmul(banks[2 + self.layer][:, 0:D], stage[:, n, :], w[:, n, :], start=(n == 0), stop=(n == parts - 1))
                mm.then_inc(self.summed, 1)

            def transposes(self, pe, t):
                pe.wait_ge(self.norm_done, t + 1)
                if not early(t, 1):
                    pe.wait_ge(self.trn_copied, t)
                pe.transpose(banks[3][:, 0:P], nrm[:, 0:P], ident[:])
                pe.transpose(banks[3][0:MUL1, P:2 * P], nrm[:, P:D], ident[:]).then_inc(self.transposed, 1)

            def linear(self, pe, t):
                pe.wait_ge(self.trn_copied, t + 1)
                if not early(t, 1):
                    pe.wait_ge(self.pre_done, t)
                dst = banks[4][:, 0:2 * D].rearrange("p (l d) -> p l d", l=2)
                pe.matmul(dst[:, :, 0:P], trn_a, lin_w[:], start=True, stop=True)
                pe.matmul(dst[:, :, P:D], trn_b, lin_wz[:], start=True, stop=True).then_inc(self.lin_done, 1)

            def residual(self, dve, t, last=None):
                dve.wait_ge(self.summed, t + 1)
                if last is None:
                    x = x_in
                    dve.wait_ge(self.x_loaded, t * 16 + 16)
                else:
                    x = x_last[self.layer][last]
                    dve.wait_ge(last_loaded[self.layer], 16 * (NT - NE))
                if not early(t, 1):
                    dve.wait_ge(self.norm_done, t)
                if self.layer == 0:
                    dve.scalar_tensor_tensor(out=res, in0=banks[2][:, 0:D], scalar=0.0, in1=x, op0=ALU.max, op1=ALU.add)\
                       .then_inc(self.half, 1)
                    dve.wait_ge(self.half, t + 1)
                    dve.tensor_tensor(res, res, x, ALU.add).then_inc(self.res_done, 1)
                    dve.wait_ge(self.res_done, t + 1)
                else:
                    dve.scalar_tensor_tensor(out=res, in0=banks[3][:, 0:D], scalar=node_attr[:, bass.ds(t, 1)], in1=x,
                                             op0=ALU.mult, op1=ALU.add).then_inc(self.half, 1)
                    dve.wait_ge(self.half, t + 1)
                dve.bn_stats(stats, res).then_inc(self.stats_done, 1)

            def variance(self, dve, t):
                wait_apart(dve, self.stats_done, t + 1)
                dve.bn_aggr(mv, stats).then_inc(self.var_done, 1)

            def normed(self, dve, t, last=None):
                dve.wait_ge(self.std_done, t + 1)
                dve.reciprocal(rstd, std).then_inc(self.rstd_done, 1)
                dve.wait_ge(self.rstd_done, t + 1)
                if not early(t, 1):
                    if self.layer == 0:
                        dve.wait_ge(self.transposed, t)
                        dve.wait_ge(self.pre_done, t)
                    elif last is None:
                        dve.wait_ge(self.rows_stored, t * 16)
                dve.tensor_scalar(self.rows_out(last), res, mv[:, 0:1], rstd, ALU.subtract, ALU.mult).then_inc(self.norm_done, 1)

            def self_interaction(self, dve, t, last=None):
                dve.wait_ge(self.y_copied, t + 1)
                if not early(t, 1) and last is None:
                    dve.wait_ge(self.rows_stored, t * 16)
                dve.scalar_tensor_tensor(out=pre_bufs[0 if last is None else 1 + last], in0=banks[4][:, D:2 * D],
                                         scalar=node_attr[:, bass.ds(t, 1)], in1=nrm, op0=ALU.mult, op1=ALU.add).then_inc(self.pre_done, 1)

            def on_sync(self, sp, t, table):
                self.load(sp, t, table)
                self.store(sp, t)

            def on_scalar(self, act, t, last=None, added=None):
                self.stage_sums(act, t, added)
                self.root(act, t)
                if self.layer == 0:
                    self.copy_transposed(act, t)
                    self.copy_y(act, t, last)

            def on_tensor(self, pe, t):
                self.sums(pe, t)
                if self.layer == 0:
                    self.transposes(pe, t)
                    self.linear(pe, t)

            def on_vector(self, dve, t, last=None):
                self.residual(dve, t, last)
                self.variance(dve, t)
                self.normed(dve, t, last)
                if self.layer == 0:
                    self.self_interaction(dve, t, last)

            def all_stored(self, engine, n):
                if self.layer == 0:
                    engine.wait_ge(self.y_stored, 16 * n)
                engine.wait_ge(self.rows_stored, 16 * n)

        class FarEdges:

            def __init__(self, name, layer, table):
                self.layer, self.table = layer, table
                (self.lists_loaded, self.rows_gathered, self.rad_in, self.hid_lin, self.hid_out, self.w_out, self.scaled_out,
                 self.operands, self.hots, self.window_summed, self.block_done) = (
                    sem(f"{name}_{n}") for n in ("lists_loaded", "rows_gathered", "rad_in", "hid_lin", "hid_out", "w_out",
                                                 "scaled_out", "operands", "hots", "window_summed", "block_done"))
                self.windows, self.blocks, self.lists = NPAD // FW, U // 2, 2 * ITERS
                lo = K * D
                assert K * 5 * FW <= 4 * K * D
                self.hot = work[:, lo:lo + K * 5 * FW].rearrange("p (k j n) -> p k j n", k=K, j=5)
                lo = 5 * K * D
                self.nodes = work[:, lo:lo + FW]
                self.far_dst = work[:, lo + FW:lo + FW + K]
                self.is_far = work[:, lo + FW + K:lo + FW + 2 * K]
                self.all_dst = work[:, lo + FW + 2 * K:lo + FW + 3 * K].bitcast(I32)

            def lists_in(self, g, b):
                return g * (16 * (self.blocks + 1)) + 16 * (b + 2)

            def on_sync(self, sp):
                with sp.Fori(0, self.lists) as g:
                    for b in range(self.blocks):
                        c = g * self.blocks + b
                        sp.wait_ge(self.block_done, c + 1)
                        if b == 0:
                            sp.dma_start(idx[0][:], a["src"][bass.ds(g, 1)].rearrange("o p t -> (o p) t")).then_inc(self.lists_loaded, 16)
                        sp.dma_start(self.all_dst, a["dst_tiles"][:, bass.ds(c * K, K)]).then_inc(self.lists_loaded, 16)
                        if self.layer == 1:
                            sp.dma_start(rad[0], a["radial"][bass.ds(c, 1)].rearrange("o p e -> (o p) e")).then_inc(self.rad_in, 16)
                        wait_apart(sp, self.lists_loaded, self.lists_in(g, b))
                sp.wait_ge(self.block_done, BLOCKS + 1)

            def on_gpsimd(self, pool):
                with pool.Fori(0, self.lists) as g:
                    for b in range(self.blocks):
                        pool.wait_ge(self.block_done, g * self.blocks + (b + 1))
                        wait_apart(pool, self.lists_loaded, self.lists_in(g, b))
                        for k in range(K):
                            t = b * K + k
                            pool.indirect_dma_start(gat[0][:, k, :], None, self.table, bass.IndirectOffsetOnAxis(idx[0][:, t:t + 1], 0))\
                                .then_inc(self.rows_gathered, 16)
                pool.wait_ge(self.block_done, BLOCKS + 1)

            def on_scalar(self, act):
                with act.Fori(0, BLOCKS) as c:
                    act.wait_ge(self.hid_lin, c + 1)
                    act.activation(hid[0], banks[2][0:NR, 0:BE], ACT.Relu, scale=RELU_SCALE).then_inc(self.hid_out, 1)
                    act.wait_ge(self.rows_gathered, c * (16 * K) + 16 * K)
                    for k in range(K):
                        ins = act.activation(edge_y[0][:, k, :], gat[0][:, k, :], ACT.Copy, scale=sh[:, bass.ds(c * K + k, 1), 0])
                    ins.then_inc(self.scaled_out, 1)
                act.wait_ge(self.block_done, BLOCKS + 1)

            def on_tensor(self, pe):
                with pe.Fori(0, BLOCKS) as c:
                    if self.layer == 1:
                        pe.wait_ge(self.rad_in, c * 16 + 16)
                        pe.matmul(banks[2][0:NR, 0:BE], fc1[:], rad[0], start=True, stop=True).then_inc(self.hid_lin, 1)
                        pe.wait_ge(self.hid_out, c + 1)
                        for k in range(K):
                            mm = pe.matmul(w_of[0][:, k, 0:NW], hid[0][:, k * P:k * P + P], fc2[:], start=True, stop=True)
                        mm.then_inc(self.w_out, 1)
                    with pe.Fori(0, self.windows) as w:
                        pe.wait_ge(self.hots, c * self.windows + w + 1)
                        block_sums(pe, self.layer, (banks[0], banks[1][:, 0:FW]), (gat, prod)[self.layer][0], self.hot).then_inc(self.window_summed, 1)
                pe.wait_ge(self.block_done, BLOCKS + 1)

            def on_vector(self, dve):
                for n in range(FW // W):
                    dve.tensor_scalar(self.nodes[:, n * W:n * W + W], iota[:], float(n * W + 1), None, ALU.add)
                dve.drain().then_inc(self.block_done, 1)
                with dve.Fori(0, BLOCKS) as c:
                    t = c * K
                    dve.wait_ge(self.rows_gathered, c * (16 * K) + 16 * K)
                    dve.tensor_scalar(self.is_far, rel[:, bass.ds(t, K)], float(W), None, ALU.is_ge)
                    dve.drain()
                    dve.scalar_tensor_tensor(out=self.far_dst, in0=self.all_dst, scalar=1.0, in1=self.is_far, op0=ALU.add, op1=ALU.mult)
                    if self.layer == 1:
                        dot_terms(dve, gat[0], t)
                        dve.drain()
                        dot_sums(dve, prod[0])
                        dve.drain()
                        dve.wait_ge(self.w_out, c + 1)
                        dve.wait_ge(self.scaled_out, c + 1)
                        weighted_rows(dve, prod[0], w_of[0], edge_y[0], gat[0])
                        weighted_dots(dve, prod[0], w_of[0])
                    dve.drain()
                    with dve.Fori(0, self.windows) as w:
                        dve.tensor_tensor(self.hot[:, :, 0, :], self.nodes.rearrange("p (o n) -> p o n", o=1).to_broadcast([P, K, FW]),
                                          self.far_dst.rearrange("p (k o) -> p k o", o=1).to_broadcast([P, K, FW]), ALU.is_equal)
                        dve.drain()
                        for j in range(self.layer, 4):
                            dve.tensor_tensor(self.hot[:, :, j + 1 - self.layer, :], self.hot[:, :, 0, :],
                                              sh[:, bass.ds(t, K), j:j + 1].to_broadcast([P, K, FW]), ALU.mult)
                        dve.tensor_scalar(self.nodes, self.nodes, float(FW), None, ALU.add)
                        dve.drain().then_inc(self.hots, 1)
                        dve.wait_ge(self.window_summed, c * self.windows + w + 1)
                        at = bass.ds(w * FW, FW)
                        dve.tensor_tensor(acc_a[:, :, at], acc_a[:, :, at], banks[0].rearrange("p (j n) -> p j n", j=4), ALU.add)
                        dve.tensor_tensor(acc_b[:, at], acc_b[:, at], banks[1][:, 0:FW], ALU.add)
                        dve.drain()
                    dve.tensor_scalar(self.nodes, self.nodes, float(-FW * self.windows), None, ALU.add)
                    dve.drain().then_inc(self.block_done, 1)

        nodes0, nodes1 = Node("nodes0", 0), Node("nodes1", 1)
        LAST = list(range(NE, NT))
        last_loaded = [sem("last_x_loaded"), sem("last_pre_loaded")]

        dst_loaded, rel_loaded, tables_loaded, weights_loaded, places_loaded = (
            sem(n) for n in ("dst_loaded", "rel_loaded", "tables_loaded", "weights_loaded", "places_loaded"))
        places_zeroed, zeros_set, acc_zeroed, acc_zeroed_dma = (sem(n) for n in ("places_zeroed", "zeros_set", "acc_zeroed", "acc_zeroed_dma"))
        iotas_set, ident_set = sem("iotas_set"), sem("ident_set")
        mins_found, bases_found, margins_found, bases_stored, bases_loaded = (
            sem(n) for n in ("mins_found", "bases_found", "margins_found", "bases_stored", "bases_loaded"))
        rel_found, far_found, measures_stored, measures_loaded, extremes_found, flags_found, flags_set = (
            sem(n) for n in ("rel_found", "far_found", "measures_stored", "measures_loaded", "extremes_found", "flags_found", "flags_set"))
        products_done, weights_scaled = sem("products_done"), sem("weights_scaled")
        idx_loaded = [[sem(f"idx{h}_loaded{n}") for h in range(2)] for n in range(2)]
        gathered = [[sem(f"gathered{n}_{s}") for s in range(U)] for n in range(2)]
        onehot_built, summed, added = ([sem(f"{m}{n}") for n in range(2)] for m in ("onehot_built", "summed", "added"))
        operands_ready = sem("operands_ready")
        rad_loaded = [sem(f"rad_loaded{s}") for s in range(U)]
        dot3_built, dot_built, scaled, hid_lin_done, hid_done, w_done, z_ready = (
            sem(n) for n in ("dot3_built", "dot_built", "scaled", "hid_lin_done", "hid_done", "w_done", "z_ready"))
        zeroed1, zeroed1_dma = sem("zeroed1"), sem("zeroed1_dma")

        used[0] = edge_y0
        dst_rows = carve(U * BE, ITERS).rearrange("p (b e) -> p b e", b=U)
        base_b = carve(BLOCKS).bitcast(I32)
        w1t, ws, w2t = carve(64, 64), carve(64, 64), carve(128, 64)
        w3t, wv, w4t, w5t = carve(64, 32), carve(32, 32), carve(128, 32), carve(128, 32)
        bmin, bmin_i, floors = carve(U, ITERS), carve(U, ITERS).bitcast(I32), carve(1, ITERS)
        least, margin, far = carve(1, ITERS), carve(1, ITERS), carve(1)
        far_row, margin_row = carve(P, 1), carve(ITERS, 1)
        extremes, found_flags = carve(2, 1), carve(4, 1)
        PLACES = 16 * 16

        def zeros_over(n):
            return zeros[:].rearrange("p (r n) -> p r n", r=1).to_broadcast([P, n, P])

        def in_tiles(t):
            return t.rearrange("p (r n) -> p r n", n=P)

        far0 = FarEdges("far0", 0, a["x"])
        far1 = FarEdges("far1", 1, y_dram)

        with nc.Block() as block:
            @block.sync
            def _(sp):
                for h in range(2):
                    sp.dma_start(idx[h][:], a["src"][h]).then_inc(idx_loaded[0][h], 16)
                sp.dma_start(dst_rows.bitcast(I32), a["dst"].rearrange("(p b e) -> p b e", p=ITERS, b=U)).then_inc(dst_loaded, 16)
                sp.dma_start(rel[:].bitcast(I32), a["dst_tiles"]).then_inc(rel_loaded, 16)
                sp.dma_start(sh[:], a["sh"]).then_inc(tables_loaded, 16)
                sp.wait_ge(bases_found, 1)
                sp.dma_start(base_dram.rearrange("(p b) -> p b", p=ITERS), bmin_i).then_inc(bases_stored, 16)
                sp.wait_ge(bases_stored, 16)
                sp.dma_start(base_b, base_dram.rearrange("(o b) -> o b", o=1).to_broadcast([P, BLOCKS])).then_inc(bases_loaded, 16)
                sp.dma_start(base_row[:], base_dram.rearrange("(o b) -> o b", o=1)).then_inc(bases_loaded, 16)

                def body(i, first, last, tile):
                    if not last:
                        refill_indices(sp, i, 0, idx_loaded[0], gathered[0])
                    if tile is not None:
                        if not early(tile, 1):
                            nodes0.store(sp, tile - 1)
                        nodes0.load(sp, tile, a["x"])
                        if last:
                            nodes0.store(sp, tile)
                    if not last:
                        refill_indices(sp, i, 1, idx_loaded[0], gathered[0])
                found = iterations(sp, body)
                is_far, late, _ = found
                for n, t in enumerate(LAST):
                    sp.dma_start(x_last[0][n], tile_rows(a["x"], t)).then_inc(last_loaded[0], 16)
                for s in range(U):
                    sp.wait_ge(gathered[0][s], ITERS * 16 * K)
                with sp.If(is_far):
                    sp.wait_ge(added[0], BLOCKS)
                    far0.on_sync(sp)
                with sp.If(late):
                    nodes0.on_sync(sp, 0, a["x"])
                    with sp.Fori(1, NE) as t:
                        nodes0.on_sync(sp, t, a["x"])
                for h in range(2):
                    sp.dma_start(idx[h][:], a["src"][h]).then_inc(idx_loaded[1][h], 16)
                for n, t in enumerate(LAST):
                    nodes0.store(sp, t, n)
                nodes0.all_stored(sp, NT)

                for q in range(U):
                    sp.dma_start(rad[q], a["radial"][q]).then_inc(rad_loaded[q], 16)

                def body(i, first, last, tile):
                    for q in range(U):
                        if not (first and q < 3) and not (last and q >= 3):
                            sp.wait_ge(hid_lin_done, i * U + (q - 2))
                            sp.dma_start(rad[(q + 3) % U], a["radial"][bass.ds(i * U + (q + 3), 1)].rearrange("o p e -> (o p) e"))\
                              .then_inc(rad_loaded[(q + 3) % U], 16)
                        if q % 3 == 2 and not last:
                            refill_indices(sp, i, q // 3, idx_loaded[1], gathered[1])
                        if q == 2 and tile is not None:
                            if not early(tile, 1):
                                nodes1.store(sp, tile - 1)
                            nodes1.load(sp, tile, pre_dram)
                    if last and tile is not None:
                        nodes1.store(sp, tile)
                iterations(sp, body, found)
                sp.wait_ge(z_ready, BLOCKS)
                for n, t in enumerate(LAST):
                    sp.dma_start(x_last[1][n], tile_rows(pre_dram, t)).then_inc(last_loaded[1], 16)
                with sp.If(is_far):
                    sp.wait_ge(added[1], BLOCKS)
                    far1.on_sync(sp)
                with sp.If(late):
                    nodes1.on_sync(sp, 0, pre_dram)
                    with sp.Fori(1, NE) as t:
                        nodes1.on_sync(sp, t, pre_dram)
                for n, t in enumerate(LAST):
                    nodes1.store(sp, t, n)
                nodes1.all_stored(sp, NT)

            @block.gpsimd
            def _(pool):
                pool.iota(iota[:], [[1, W]], base=0, channel_multiplier=0, allow_small_or_imprecise_dtypes=True)
                pool.iota(floors, [[0, 1]], base=-P * (EARLY - 1), channel_multiplier=P,
                          allow_small_or_imprecise_dtypes=True).then_inc(iotas_set, 1)
                pool.memset(ident[:], 0.0).then_inc(ident_set, 1)
                pool.wait_ge(ident_set, 1)
                pool.affine_select(out=ident[:], in_=ident[:], compare_op=ALU.not_equal, fill=1.0, base=0,
                                   pattern=[[-1, P]], channel_multiplier=1).then_inc(ident_set, 1)

                def body(i, first, last, tile):
                    for q in range(U):
                        gather_block(pool, i, q, first, a["x"], idx_loaded[0], gathered[0], summed[0])
                found = iterations(pool, body)
                is_far, late, _ = found
                with pool.If(is_far):
                    pool.wait_ge(added[0], BLOCKS)
                    far0.on_gpsimd(pool)
                pool.wait_ge(nodes0.staged, NT)
                pool.memset(acc_b[:], 0.0).then_inc(zeroed1, 1)
                nodes0.all_stored(pool, NT)

                def body(i, first, last, tile):
                    for q in range(U):
                        gather_block(pool, i, q, first, y_dram, idx_loaded[1], gathered[1], summed[1])
                iterations(pool, body, found)
                with pool.If(is_far):
                    pool.wait_ge(added[1], BLOCKS)
                    far1.on_gpsimd(pool)

            @block.scalar
            def _(act):
                act.preload_act_table(ACT.Sqrt)
                for dst, src in ((w1t, "W1t"), (ws, "Ws"), (w3t, "W3t"), (wv, "Wv")):
                    act.dma_start(dst, a[src]).then_inc(weights_loaded, 16)
                for r in range(4):
                    for dst, src in ((w2t, "W2t"), (w4t, "W4t"), (w5t, "W5t")):
                        act.dma_start(dst[:, 32 * r:32 * r + 32], a[src]).then_inc(weights_loaded, 16)
                act.wait_ge(zeros_set, 1)
                act.dma_start(in_tiles(acc_a[:, 0, :]), zeros_over(NT)).then_inc(acc_zeroed_dma, 16)
                act.dma_start(in_tiles(acc_b[:]), zeros_over(NT)).then_inc(acc_zeroed_dma, 16)
                for part in (1, 2):
                    act.activation(in_tiles(acc_a[:, part, :]), zeros_over(NT), ACT.Copy).then_inc(acc_zeroed, 1)
                act.dma_start(node_attr[:], a["node_attr"]).then_inc(tables_loaded, 16)
                act.dma_start(fc1[:], a["fc1"]).then_inc(tables_loaded, 16)
                act.dma_start(fc2[:], a["fc2"]).then_inc(tables_loaded, 16)
                act.wait_ge(places_zeroed, 1)
                for n, (s, v) in enumerate((("W_l1_0", "W_l1_1"), ("W_si0", "W_si1"))):
                    act.dma_start(lin_w[0:64, n, 0:64], a[s]).then_inc(places_loaded, 16)
                    act.dma_start(lin_w[64:96, n, 64:96], a[v]).then_inc(places_loaded, 16)
                    act.dma_start(lin_w[96:128, n, 96:128], a[v]).then_inc(places_loaded, 16)
                    act.dma_start(lin_wz[:, n, :], a[v]).then_inc(places_loaded, 16)
                act.dma_start(sum_w[0:64, 0, 0:64], a["W_l2_00"]).then_inc(places_loaded, 16)
                for i in range(3):
                    lo = MUL0 + MUL1 * i
                    rows, part = ((slice(64, 128), 0), (slice(0, 64), 1), (slice(64, 128), 1))[i]
                    act.dma_start(sum_w[rows, part, lo:lo + 32], a["W_l2_01"]).then_inc(places_loaded, 16)
                    act.dma_start(sum_w[32 * i:32 * i + 32, 2, lo:lo + 32], a["W_l2_11"]).then_inc(places_loaded, 16)
                act.dma_start(sum_w[96:128, 2, 0:64], a["W_l2_10"]).then_inc(places_loaded, 16)
                act.wait_ge(margins_found, 1)
                act.wait_ge(far_found, 1)
                act.dma_start(measures_dram[0].rearrange("(p o) -> p o", o=1), far).then_inc(measures_stored, 16)
                act.dma_start(measures_dram[1, 0:ITERS].rearrange("(p o) -> p o", o=1), margin).then_inc(measures_stored, 16)
                act.wait_ge(measures_stored, 32)
                act.dma_start(far_row, measures_dram[0].rearrange("(o p) -> o p", o=1)).then_inc(measures_loaded, 16)
                act.dma_start(margin_row, measures_dram[1, 0:ITERS].rearrange("(o p) -> o p", o=1)).then_inc(measures_loaded, 16)
                act.wait_ge(products_done, 1)
                act.wait_ge(places_zeroed, 1)
                g1, g2, g3, g4, g5 = banks[2:7]
                c2, c5 = C0 * INV3 * LIN_S, C1 * INV6 * LIN_V
                c34 = C1 * INV3 * LIN_V
                v0, v1, j = slice(64, 96), slice(96, 128), [slice(32 * q, 32 * q + 32) for q in range(4)]
                s_, hs, hv = slice(0, 64), slice(0, 64), [slice(64 + 32 * i, 96 + 32 * i) for i in range(3)]
                places = [
                    (0, s_, hs, g1, C0 * LIN_S), (0, v0, hv[0], g4, c34), (0, v1, hv[1], g4, c34),
                    (1, s_, hv[0], g3, c34), (1, v0, hs, g2, c2), (1, v1, hv[2], g5, -c5),
                    (2, s_, hv[1], g3, c34), (2, v0, hv[2], g5, c5), (2, v1, hs, g2, c2),
                    (3, s_, hv[2], g3, c34), (3, v0, hv[1], g5, -c5), (3, v1, hv[0], g5, c5),
                    (4, j[0], hv[2], g4, c34), (4, j[1], hv[1], g5, c5), (4, j[2], hv[0], g5, -c5), (4, j[3], hs, g2, c2),
                ]
                for part, rows, cols, g, c in places:
                    act.activation(msg_w[rows, part, cols], g[rows, 0:cols.stop - cols.start], ACT.Copy, scale=float(c))
                act.wait_ge(places_loaded, PLACES)
                act.activation(lin_w[0:64], lin_w[0:64], ACT.Copy, scale=float(LIN_S))
                act.activation(lin_w[64:128], lin_w[64:128], ACT.Copy, scale=float(LIN_V))
                act.activation(lin_wz[:], lin_wz[:], ACT.Copy, scale=float(LIN_V))
                act.activation(sum_w[:], sum_w[:], ACT.Copy, scale=SUM_SCALE).then_inc(weights_scaled, 1)
                act.wait_ge(weights_scaled, 1)
                act.activation(sum_w[96:128, 2, 0:64], sum_w[96:128, 2, 0:64], ACT.Copy, scale=float(INV3)).then_inc(weights_scaled, 1)
                act.wait_ge(weights_scaled, 2)
                act.wait_ge(tables_loaded, 16 * 4)

                found = load_flags(act)
                is_far, late, in_order = found
                with act.If(in_order):
                    nodes0.on_scalar(act, 0, added=(added[0], EARLY * U))
                    with act.Fori(1, NE) as t:
                        nodes0.on_scalar(act, t, added=(added[0], t * U + EARLY * U))
                with act.If(is_far):
                    act.wait_ge(far0.block_done, BLOCKS + 1)
                with act.If(late):
                    act.wait_ge(added[0], BLOCKS)
                    nodes0.on_scalar(act, 0)
                    with act.Fori(1, NE) as t:
                        nodes0.on_scalar(act, t)
                for n, t in enumerate(LAST):
                    nodes0.stage_sums(act, t, (added[0], BLOCKS))
                    if n == len(LAST) - 1:
                        act.wait_ge(nodes0.staged, NT)
                        act.dma_start(in_tiles(acc_a[:, 0, :]), zeros_over(NT)).then_inc(zeroed1_dma, 16)
                    if n:
                        nodes0.copy_transposed(act, t - 1)
                        nodes0.copy_y(act, t - 1, n - 1)
                    nodes0.root(act, t)
                nodes0.copy_transposed(act, LAST[-1])
                nodes0.copy_y(act, LAST[-1], len(LAST) - 1)
                act.activation(in_tiles(acc_a[:, 1, :]), zeros_over(NT), ACT.Copy).then_inc(zeroed1, 1)

                def relu(c, s):
                    act.wait_ge(hid_lin_done, c + 1)
                    if not early(c, 2):
                        act.wait_ge(w_done, c - 1)
                    act.activation(hid[s], banks[2][0:NR, 0:BE], ACT.Relu, scale=RELU_SCALE).then_inc(hid_done, 1)

                relu(0, 0)

                def body(i, first, last, tile):
                    for q in range(U):
                        c, s = i * U + q, q % 2
                        if not (last and q == U - 1):
                            relu(c + 1, 1 - s)
                        act.wait_ge(gathered[1][q], i * (16 * K) + 16 * K)
                        if not early(c, 2):
                            act.wait_ge(z_ready, c - 1)
                        for k in range(K):
                            ins = act.activation(edge_y[s][:, k, :], gat[q][:, k, :], ACT.Copy,
                                                 scale=sh[:, bass.ds(i * (U * K) + (q * K + k), 1), 0])
                        ins.then_inc(scaled, 1)
                        if tile is not None and q == 1:
                            nodes1.stage_sums(act, tile, (added[1], i * U))
                        if tile is not None and q == 4:
                            nodes1.root(act, tile)
                iterations(act, body, found)
                with act.If(is_far):
                    act.wait_ge(added[1], BLOCKS)
                    far1.on_scalar(act)
                with act.If(late):
                    act.wait_ge(added[1], BLOCKS)
                    nodes1.on_scalar(act, 0)
                    with act.Fori(1, NE) as t:
                        nodes1.on_scalar(act, t)
                for n, t in enumerate(LAST):
                    nodes1.on_scalar(act, t, n, (added[1], BLOCKS))

            @block.tensor
            def _(pe):
                pe.wait_ge(weights_loaded, 16 * 16)
                pe.matmul(banks[2][0:64, 0:64], w1t, ws, start=True, stop=True)
                pe.matmul(banks[3][:, 0:64], w2t, ws, start=True, stop=True)
                pe.matmul(banks[4][0:64, 0:32], w3t, wv, start=True, stop=True)
                pe.matmul(banks[5][:, 0:32], w4t, wv, start=True, stop=True)
                pe.matmul(banks[6][:, 0:32], w5t, wv, start=True, stop=True).then_inc(products_done, 1)
                pe.wait_ge(ident_set, 2)

                def body(i, first, last, tile):
                    for q in range(U):
                        c, s = i * U + q, q % 2
                        pe.wait_ge(operands_ready, c + 1)
                        if not early(c, 2):
                            pe.wait_ge(added[0], c - 1)
                        pe.wait_ge(gathered[0][q], i * (16 * K) + 16 * K)
                        block_sums(pe, 0, sum_bank(s), gat[q], hot[s]).then_inc(summed[0], 1)
                        if tile is not None:
                            if q == 1:
                                nodes0.sums(pe, tile)
                            if q == 3:
                                nodes0.transposes(pe, tile)
                            if q == 4:
                                nodes0.linear(pe, tile)
                found = iterations(pe, body)
                is_far, late, _ = found
                with pe.If(is_far):
                    far0.on_tensor(pe)
                with pe.If(late):
                    nodes0.on_tensor(pe, 0)
                    with pe.Fori(1, NE) as t:
                        nodes0.on_tensor(pe, t)
                for n, t in enumerate(LAST):
                    nodes0.sums(pe, t)
                    if n:
                        nodes0.transposes(pe, t - 1)
                        nodes0.linear(pe, t - 1)
                nodes0.transposes(pe, LAST[-1])
                nodes0.linear(pe, LAST[-1])

                def hidden(c, q, uses):
                    pe.wait_ge(rad_loaded[q], uses * 16)
                    if not early(c, 1):
                        pe.wait_ge(hid_done, c)
                    pe.matmul(banks[2][0:NR, 0:BE], fc1[:], rad[q], start=True, stop=True).then_inc(hid_lin_done, 1)

                def sums(c, s):
                    pe.wait_ge(z_ready, c + 1)
                    if not early(c, 2):
                        pe.wait_ge(added[1], c - 1)
                    block_sums(pe, 1, sum_bank(s), prod[s], hot[s]).then_inc(summed[1], 1)

                hidden(0, 0, 1)

                def body(i, first, last, tile):
                    for q in range(U):
                        c, s = i * U + q, q % 2
                        if not (last and q == U - 1):
                            hidden(c + 1, (q + 1) % U, i + 1 + (q + 1) // U)
                        pe.wait_ge(hid_done, c + 1)
                        if not early(c, 2):
                            pe.wait_ge(z_ready, c - 1)
                        for k in range(K):
                            mm = pe.matmul(w_of[s][:, k, 0:NW], hid[s][:, k * P:k * P + P], fc2[:], start=True, stop=True)
                        mm.then_inc(w_done, 1)
                        if not early(c, 1):
                            sums(c - 1, 1 - s)
                        if tile is not None and q == 3:
                            nodes1.sums(pe, tile)
                iterations(pe, body, found)
                sums(BLOCKS - 1, 1)
                with pe.If(is_far):
                    pe.wait_ge(added[1], BLOCKS)
                    far1.on_tensor(pe)
                with pe.If(late):
                    nodes1.on_tensor(pe, 0)
                    with pe.Fori(1, NE) as t:
                        nodes1.on_tensor(pe, t)
                for t in LAST:
                    nodes1.sums(pe, t)

            @block.vector
            def _(dve):
                dve.memset(zeros[:], 0.0).then_inc(zeros_set, 1)
                dve.memset(lin_w[:], 0.0)
                dve.memset(sum_w[:], 0.0)
                dve.memset(msg_w[:], 0.0)
                dve.memset(eps[:], EPS).then_inc(places_zeroed, 1)
                dve.wait_ge(dst_loaded, 16)
                dve.tensor_reduce(bmin, dst_rows.bitcast(I32), AX.X, ALU.min).then_inc(mins_found, 1)
                dve.wait_ge(mins_found, 1)
                dve.tensor_scalar(bmin_i, bmin, float(NPAD - W), None, ALU.min).then_inc(bases_found, 1)
                dve.wait_ge(bases_found, 1)
                dve.tensor_reduce(least, bmin_i, AX.X, ALU.min).then_inc(mins_found, 1)
                dve.wait_ge(mins_found, 2)
                dve.wait_ge(iotas_set, 1)
                dve.tensor_tensor(margin, least, floors, ALU.subtract).then_inc(margins_found, 1)
                dve.memset(acc_a[:, 3, :], 0.0)
                dve.wait_ge(rel_loaded, 16)
                dve.wait_ge(bases_loaded, 32)
                rel_k = rel[:].rearrange("p (b k) -> p b k", k=K)
                dve.tensor_tensor(rel_k, rel_k.bitcast(I32), base_b.rearrange("p (b o) -> p b o", o=1)
                                  .to_broadcast([P, BLOCKS, K]), ALU.subtract).then_inc(rel_found, 1)
                dve.wait_ge(rel_found, 1)
                dve.tensor_reduce(far, rel[:], AX.X, ALU.max).then_inc(far_found, 1)
                dve.wait_ge(tables_loaded, 16 * 4)

                def set_flags():
                    dve.wait_ge(measures_loaded, 32)
                    dve.tensor_reduce(extremes[:, 0:1], far_row, AX.X, ALU.max)
                    dve.tensor_reduce(extremes[:, 1:2], margin_row, AX.X, ALU.min).then_inc(extremes_found, 1)
                    dve.wait_ge(extremes_found, 1)
                    dve.tensor_scalar(found_flags[:, 0:1], extremes[:, 0:1], float(W), None, ALU.is_ge)
                    dve.tensor_scalar(found_flags[:, 1:2], extremes[:, 1:2], 0.0, None, ALU.is_lt)
                    dve.tensor_scalar(found_flags[:, 2:3], extremes[:, 0:1], float(W), None, ALU.is_lt)
                    dve.tensor_scalar(found_flags[:, 3:4], extremes[:, 1:2], 0.0, None, ALU.is_ge).then_inc(flags_found, 1)
                    dve.wait_ge(flags_found, 1)
                    dve.tensor_copy(flags[:, 0:1], found_flags[:, 0:1])
                    dve.tensor_tensor(flags[:, 1:2], found_flags[:, 0:1], found_flags[:, 1:2], ALU.max)
                    dve.tensor_tensor(flags[:, 2:3], found_flags[:, 2:3], found_flags[:, 3:4], ALU.min).then_inc(flags_set, 1)

                def body(i, first, last, tile):
                    for q in range(U):
                        c, s = i * U + q, q % 2
                        t = i * (U * K) + q * K
                        if not early(c, 2):
                            dve.wait_ge(summed[0], c - 1)
                        onehots(dve, hot[s], t).then_inc(onehot_built[0], 1)
                        dve.wait_ge(onehot_built[0], c + 1)
                        dve.tensor_tensor(hot[s][:, :, 1:5, :], hot[s][:, :, 0:1, :].to_broadcast([P, K, 4, W]), attr(t, 0, 4),
                                          ALU.mult).then_inc(operands_ready, 1)
                        if q == 0:
                            bases = load_bases(0, U - 1) if first else load_bases(i * U - 1, U)
                        if early(c, 2) and q == 1:
                            dve.wait_ge(acc_zeroed, 2)
                            dve.wait_ge(acc_zeroed_dma, 32)
                        if tile is not None and q == 3:
                            nodes0.normed(dve, tile)
                        if not early(c, 1):
                            add_sums(dve, c, banks[1 - s], bases[q - first], summed[0], added[0])
                        if tile is not None:
                            if q == 2:
                                nodes0.residual(dve, tile)
                                nodes0.variance(dve, tile)
                            if q == 5:
                                nodes0.self_interaction(dve, tile)
                    if first:
                        set_flags()
                    if last:
                        add_sums(dve, BLOCKS, banks[1], load_bases(BLOCKS - 1, 1)[0], summed[0], added[0])
                found = iterations(dve, body)
                is_far, late, _ = found
                with dve.If(is_far):
                    far0.on_vector(dve)
                with dve.If(late):
                    nodes0.on_vector(dve, 0)
                    with dve.Fori(1, NE) as t:
                        nodes0.on_vector(dve, t)
                for n, t in enumerate(LAST):
                    nodes0.residual(dve, t, n)
                    nodes0.variance(dve, t)
                    if n:
                        nodes0.self_interaction(dve, t - 1, n - 1)
                    nodes0.normed(dve, t)
                nodes0.self_interaction(dve, LAST[-1], len(LAST) - 1)

                for part in (2, 3):
                    dve.memset(acc_a[:, part, :], 0.0)

                def body(i, first, last, tile):
                    for q in range(U):
                        c, s = i * U + q, q % 2
                        t = i * (U * K) + q * K
                        if not early(c, 2):
                            dve.wait_ge(summed[1], c - 1)
                        onehots(dve, hot[s], t).then_inc(onehot_built[1], 1)
                        dve.wait_ge(gathered[1][q], i * (16 * K) + 16 * K)
                        if not early(c, 1):
                            dve.wait_ge(dot_built, c)
                        dot_terms(dve, gat[q], t).then_inc(dot3_built, 1)
                        dve.wait_ge(onehot_built[1], c + 1)
                        dve.tensor_tensor(hot[s][:, :, 1:4, :], hot[s][:, :, 0:1, :].to_broadcast([P, K, 3, W]), attr(t, 1, 4), ALU.mult)
                        dve.wait_ge(dot3_built, c + 1)
                        dot_sums(dve, prod[s]).then_inc(dot_built, 1)
                        if q == 0:
                            bases = load_bases(0, U - 1) if first else load_bases(i * U - 1, U)
                        dve.wait_ge(w_done, c + 1)
                        dve.wait_ge(scaled, c + 1)
                        weighted_rows(dve, prod[s], w_of[s], edge_y[s], gat[q])
                        dve.wait_ge(dot_built, c + 1)
                        weighted_dots(dve, prod[s], w_of[s]).then_inc(z_ready, 1)
                        if early(c, 2) and q == 1:
                            dve.wait_ge(zeroed1, 2)
                            dve.wait_ge(zeroed1_dma, 16)
                        if not early(c, 1):
                            add_sums(dve, c, banks[1 - s], bases[q - first], summed[1], added[1])
                        if tile is not None:
                            if q == 4:
                                nodes1.residual(dve, tile)
                                nodes1.variance(dve, tile)
                            if q == 5:
                                nodes1.normed(dve, tile)
                    if last:
                        add_sums(dve, BLOCKS, banks[1], load_bases(BLOCKS - 1, 1)[0], summed[1], added[1])
                iterations(dve, body, found)
                with dve.If(is_far):
                    far1.on_vector(dve)
                with dve.If(late):
                    nodes1.on_vector(dve, 0)
                    with dve.Fori(1, NE) as t:
                        nodes1.on_vector(dve, t)
                for n, t in enumerate(LAST):
                    nodes1.on_vector(dve, t, n)


def kernel(**inputs):
    import concourse.bacc as _bacc
    from concourse.bass_utils import run_bass_kernel_spmd as _run

    arr = {k: np.asarray(v) for k, v in inputs.items()}
    order = np.concatenate([np.arange(MUL0), (MUL0 + 3 * np.arange(MUL1)[None, :] + np.arange(3)[:, None]).reshape(-1)])
    back = np.argsort(order)

    def edges(v, fill=0):
        return np.concatenate([v, np.full((EPAD - E,) + v.shape[1:], fill, v.dtype)])

    def by_tile(v):
        return np.ascontiguousarray(v.reshape((TILES, P) + v.shape[1:]).swapaxes(0, 1))

    dst, src = edges(arr["dst"], N - 1), edges(arr["src"])
    nodes = {"x": arr["x"][:, order], "node_attr": arr["node_vec1"]}
    nodes = {k: np.concatenate([v, np.zeros((NPAD - N,) + v.shape[1:], v.dtype)]) for k, v in nodes.items()}
    arrays = {
        "x": nodes["x"],
        "node_attr": nodes["node_attr"].reshape(NT, P).T,
        "dst": dst, "dst_tiles": by_tile(dst),
        "src": src.reshape(2 * ITERS, H, P).swapaxes(1, 2),
        "sh": by_tile(edges(arr["edge_attr_4"])),
        "radial": edges(arr["edge_attr_10"]).reshape(BLOCKS, BE, NB).swapaxes(1, 2),
        "W1t": arr["L0_gnn_W1"].T, "W2t": arr["L0_gnn_W2"].T, "W3t": arr["L0_gnn_W3"].T,
        "W4t": arr["L0_gnn_W4"].T, "W5t": arr["L0_gnn_W5"].T, "Ws": arr["L0_gnn_Ws"], "Wv": arr["L0_gnn_Wv"],
        "fc1": arr["L1_gnn_W_fc1"], "fc2": arr["L1_gnn_W_fc2"],
    }
    for k in ("W_si0", "W_si1", "W_l1_0", "W_l1_1", "W_l2_00", "W_l2_10", "W_l2_01", "W_l2_11"):
        arrays[k] = arr["L1_gnn_" + k]
    arrays = {k: np.ascontiguousarray(v) for k, v in arrays.items()}
    nc = _bacc.Bacc("TRN2", target_bir_lowering=False, num_devices=1)
    args = {k: nc.dram_tensor("in_" + k, v.shape, mybir.dt.from_np(v.dtype), kind="ExternalInput").ap() for k, v in arrays.items()}
    out = nc.dram_tensor("out_rows", (N, D), F32, kind="ExternalOutput").ap()
    build(nc, args, out)
    r = _run(nc, [{"in_" + k: v for k, v in arrays.items()}], core_ids=[0])
    return r.results[0]["out_rows"][:, back]
```

```python
from collections import namedtuple
from contextlib import ExitStack

import numpy as np

import concourse.bass as bass
from concourse import mybir

F32 = mybir.dt.float32
I32 = mybir.dt.int32
BF16 = mybir.dt.bfloat16
ALU = mybir.AluOpType
ACT = mybir.ActivationFunctionType
AX = mybir.AxisListType
DVE = mybir.EngineType.DVE

P = 128
N, E = 6250, 200000
MUL0, MUL1 = 64, 32
D = MUL0 + 3 * MUL1
NB, NR = 10, 100
NW = 2 * MUL0 + 2 * MUL1
ZW = 2 * MUL0 + 6 * MUL1
NT = -(-N // P)
NPAD = NT * P
K = 3
BE = K * P
W = 32
U = 6
H = U // 2 * K
ITERS = -(-E // (BE * U))
BLOCKS = ITERS * U
TILES = BLOCKS * K
EPAD = TILES * P
RP = 16 * U
RN = U * BE * NB // RP
FW = P
EARLY = 40
NE = ITERS - EARLY

EPS = 1e-5
C0 = 1.0 / np.sqrt(MUL0 + MUL1)
C1 = np.sqrt(3.0 / (MUL0 + 2 * MUL1))
INV3, INV6 = 1.0 / np.sqrt(3.0), 1.0 / np.sqrt(6.0)
LIN_S, LIN_V = 1.0 / np.sqrt(MUL0), 1.0 / np.sqrt(MUL1)
RELU_SCALE = float(np.sqrt(2.0) / np.sqrt(NB))
SUM_SCALE = float(0.5 / np.sqrt(MUL0 + MUL1) / np.sqrt(16.0) / np.sqrt(NR))

TileBuffers = namedtuple("TileBuffers", "stage x res nrm y pre trn_a trn_b stats mv std rstd")


def build(nc, a, out):
    with ExitStack() as ctx:
        def sb(name, shape, dt=F32):
            return ctx.enter_context(nc.sbuf_tensor(name, shape, dt))

        def sem(name):
            return ctx.enter_context(nc.semaphore(name))

        def dram(name, shape, dt=F32):
            return nc.dram_tensor(name, shape, dt).ap()

        acc_a = sb("acc_a", [P, 4, NPAD])
        acc_b = sb("acc_b", [P, NPAD])
        sh = sb("sh", [P, TILES, 4])
        rel = sb("rel", [P, TILES])
        iota = sb("iota", [P, W])
        ident = sb("ident", [P, P])
        base_row = sb("base_row", [1, BLOCKS], I32)
        flags = sb("flags", [1, 3], I32)
        node_attr = sb("node_attr", [P, NT])
        msg_w = sb("msg_w", [P, 5, D])
        lin_w = sb("lin_w", [P, 2, P])
        lin_wz = sb("lin_wz", [MUL1, 2, MUL1])
        sum_w = sb("sum_w", [P, 3, D])
        fc1 = sb("fc1", [6 * NB, NR], BF16)
        fc2 = sb("fc2", [NR, NW])
        idx = [sb(f"idx{h}", [P, H], I32) for h in range(2)]
        eps = sb("eps", [P, 1])
        zeros = sb("zeros", [P, P])

        ROOM = 11248
        work = sb("work", [P, ROOM])
        used = [0]

        def carve(cols, parts=P):
            lo = used[0]
            used[0] += cols
            assert used[0] <= ROOM
            return work[0:parts, lo:lo + cols]

        def by_edge_tile(cols):
            return carve(K * cols).rearrange("p (k d) -> p k d", k=K)

        gat = [by_edge_tile(D) for _ in range(U)]
        hot_lo = used[0]
        hot = [carve(K * 5 * W).rearrange("p (k j n) -> p k j n", k=K, j=5) for _ in range(2)]
        prod0 = used[0]
        prod = [by_edge_tile(ZW) for _ in range(2)]

        def carve_tile(stage, trn):
            return TileBuffers(stage, *(carve(D) for _ in range(5)), *trn, carve(6), carve(2), carve(1), carve(1))

        stage, trn = carve(5 * P).rearrange("p (a n) -> p a n", a=5), (carve(P), carve(P, MUL1))
        in_loop = carve_tile(stage, trn)
        rad_in, rad_rest = carve(RN, RP), carve(RN, RP)
        rad_parts = carve(3 * RN // 2, RP).bitcast(BF16).rearrange("p (m n) -> p m n", m=3)
        shared0 = used[0]
        hid = [carve(BE, NR) for _ in range(2)]
        rad = [carve(BE // 2, 6 * NB).bitcast(BF16) for _ in range(U)]
        after_loop = []
        for n in range(NT - NE):
            used[0] = prod0 + n * 5 * P
            stage = carve(5 * P).rearrange("p (a n) -> p a n", a=5)
            assert used[0] <= prod0 + 2 * K * ZW
            used[0] = hot_lo + n * 2 * P
            trn = (carve(P), carve(P, MUL1))
            assert used[0] <= hot_lo + 2 * K * 5 * W
            used[0] = n * (5 * D + 10)
            after_loop.append(carve_tile(stage, trn))
            assert used[0] <= U * K * D

        psum_all = ctx.enter_context(nc.psum_tensor("psum_all", [P, 8, 512], F32))
        banks = [psum_all[:, n, :] for n in range(8)]
        w_of = [psum_all[:, 4 + 2 * s:6 + 2 * s, :].rearrange("p b (h d) -> p (b h) d", h=2)[:, 0:K, :] for s in range(2)]

        base_dram = dram("base_dram", [BLOCKS], I32)
        rad_dram = dram("rad_dram", [BLOCKS, 3, NB, BE], BF16)
        fc1_dram = dram("fc1_dram", [3, NB, NR], BF16)
        measures_dram = dram("measures_dram", [2, P])
        y_dram = dram("y_dram", [NPAD, D])
        pre_dram = dram("pre_dram", [NPAD, D])
        passed = sem("passed")

        def early(m, n):
            return isinstance(m, int) and m < n

        def wait_apart(engine, semaphore, value):
            engine.wait_ge(semaphore, value)
            if not isinstance(value, int):
                engine.sem_inc(passed, 1)

        def load_bases(start, n):
            _, values = nc.values_load_multi_w_load_instructions(
                base_row[0:1, bass.ds(start, n)], engines=[DVE], min_val=0, max_val=NPAD - W,
                skip_runtime_bounds_check_because="the bases are held to 0 .. NPAD - W")
            return values

        def load_flags(engine):
            engine.wait_ge(flags_set, 1)
            return [engine.value_load(flags[0:1, n:n + 1], min_val=0, max_val=1) for n in range(3)]

        def iterations(engine, body, found=None, before_flags=lambda: None):
            body(0, True, False, None)
            with engine.Fori(1, EARLY) as i:
                body(i, False, False, None)
            before_flags()
            found = found or load_flags(engine)
            _, late, in_order = found
            with engine.If(in_order):
                body(EARLY, False, False, 0)
                with engine.Fori(EARLY + 1, ITERS - 1) as i:
                    body(i, False, False, i - EARLY)
                body(ITERS - 1, False, True, NE - 1)
            with engine.If(late):
                with engine.Fori(EARLY, ITERS - 1) as i:
                    body(i, False, False, None)
                body(ITERS - 1, False, True, None)
            return found

        def refill_indices(sp, i, h, loaded, landed):
            for s in range(3 * h, 3 * h + 3):
                sp.wait_ge(landed[s], i * (16 * K) + 16 * K)
            sp.dma_start(idx[h][:], a["src"][bass.ds(i * 2 + (2 + h), 1)].rearrange("o p t -> (o p) t")).then_inc(loaded[h], 16)

        def gather_block(pool, i, q, first, table, loaded, landed, freed):
            h = q // 3
            if q % 3 == 0:
                wait_apart(pool, loaded[h], i * 16 + 16)
            if not first:
                wait_apart(pool, freed, i * U + (q + 1 - U))
            for k in range(K):
                t = q % 3 * K + k
                pool.indirect_dma_start(gat[q][:, k, :], None, table, bass.IndirectOffsetOnAxis(idx[h][:, t:t + 1], 0)).then_inc(landed[q], 16)

        def attr(t):
            return sh[:, bass.ds(t, K), :].rearrange("p k (j o) -> p k j o", o=1).to_broadcast([P, K, 4, W])

        def onehots(dve, dst, t):
            return dve.tensor_tensor(dst[:, :, 0, :], iota[:].rearrange("p (o n) -> p o n", o=1).to_broadcast([P, K, W]),
                                     rel[:, bass.ds(t, K)].rearrange("p (k o) -> p k o", o=1).to_broadcast([P, K, W]), ALU.is_equal)

        def scaled_onehots(dve, dst, t, built, c):
            dve.wait_ge(built, c + 1)
            return dve.tensor_tensor(dst[:, :, 1:5, :], dst[:, :, 0:1, :].to_broadcast([P, K, 4, W]), attr(t), ALU.mult)

        def split(dve, src, rest, parts, steps, m, n):
            if m:
                dve.wait_ge(steps[m - 1], n)
            if m == 0:
                ins = dve.tensor_copy(parts[:, 0, :], src)
            elif m == 1:
                ins = dve.tensor_tensor(rest, src, parts[:, 0, :], ALU.subtract)
            elif m == 2:
                ins = dve.tensor_copy(parts[:, 1, :], rest)
            else:
                ins = dve.tensor_tensor(parts[:, 2, :], rest, parts[:, 1, :], ALU.subtract)
            ins.then_inc(steps[m], 1)

        def load_radial(sp, dst, c, semaphore):
            for lo, n in ((0, 3), (3, 2), (5, 1)):
                sp.dma_start(dst[lo * NB:(lo + n) * NB, :], rad_dram[bass.ds(c, 1), 0:n].rearrange("o m b e -> (o m b) e"))\
                  .then_inc(semaphore, 16)

        def weighted_rows(dve, z, w, y):
            dve.tensor_tensor(z[:, :, 0:P].rearrange("p k (l u) -> p k l u", l=2), w[:, :, 0:P].rearrange("p k (l u) -> p k l u", l=2),
                              y[:, :, 0:MUL0].rearrange("p k (l u) -> p k l u", l=1).to_broadcast([P, K, 2, MUL0]), ALU.mult)
            for n in range(2):
                lo, wl = P + 96 * n, P + MUL1 * n
                ins = dve.tensor_tensor(z[:, :, lo:lo + 96].rearrange("p k (i u) -> p k i u", i=3),
                                        w[:, :, wl:wl + MUL1].rearrange("p k (i u) -> p k i u", i=1).to_broadcast([P, K, 3, MUL1]),
                                        y[:, :, MUL0:D].rearrange("p k (i u) -> p k i u", i=3), ALU.mult)
            return ins

        def block_sums(pe, layer, bank, rows, hots):
            for k in range(K):
                pe.matmul(bank[0].rearrange("p (j n) -> p j n", j=4), rows[:, k, 0:P], hots[:, k, 1:5, :], start=(k == 0), stop=(k == K - 1))
            if layer == 0:
                for j in range(4):
                    for k in range(K):
                        mm = pe.matmul(bank[1][32 * j:32 * j + 32, :], rows[:, k, P:D], hots[:, k, 1 + j, :], start=(k == 0), stop=(k == K - 1))
            else:
                for k in range(K):
                    pe.matmul(bank[1][0:96, :], rows[:, k, P:P + 96], hots[:, k, 1, :], start=(k == 0), stop=(k == K - 1))
                for i in range(3):
                    for k in range(K):
                        lo = P + 96 + MUL1 * i
                        mm = pe.matmul(bank[1][96:128, :], rows[:, k, lo:lo + MUL1], hots[:, k, 2 + i, :],
                                       start=(i == 0 and k == 0), stop=(i == 2 and k == K - 1))
            return mm

        def sum_bank(s):
            return banks[s][:, 0:4 * W], banks[s][:, 4 * W:5 * W]

        def add_sums(dve, c, bank, base, summed, added):
            dve.wait_ge(summed, c)
            if not early(c, 2):
                dve.wait_ge(added, c - 1)
            dst = acc_a[:, :, bass.ds(base, W)]
            dve.tensor_tensor(dst, dst, bank[:, 0:4 * W].rearrange("p (j n) -> p j n", j=4), ALU.add)
            dst = acc_b[:, bass.ds(base, W)]
            dve.tensor_tensor(dst, dst, bank[:, 4 * W:5 * W], ALU.add).then_inc(added, 1)

        def tile_rows(t, n):
            return t[bass.ds(n * P, P), :]

        class Node:

            def __init__(self, name, layer):
                self.layer = layer
                (self.staged, self.summed, self.half, self.res_done, self.stats_done, self.var_done, self.std_done, self.rstd_done,
                 self.norm_done, self.x_loaded, self.rows_stored) = (sem(f"{name}_{n}") for n in (
                     "staged", "summed", "half", "res_done", "stats_done", "var_done", "std_done", "rstd_done", "norm_done",
                     "x_loaded", "rows_stored"))
                if layer == 0:
                    self.transposed, self.trn_copied, self.lin_done, self.y_copied, self.pre_done, self.y_stored = (
                        sem(f"{name}_{n}") for n in ("transposed", "trn_copied", "lin_done", "y_copied", "pre_done", "y_stored"))

            def buffers(self, last):
                return in_loop if last is None else after_loop[last]

            def sum_rows(self, last):
                return banks[(2, 3)[self.layer] if last in (None, 0) else 4 + last][:, 0:D]

            def trn_bank(self, last):
                return banks[3 if last in (None, 0, 2) else 7]

            def lin_rows(self, last):
                return banks[4 if last in (None, 0) else last - 1][:, 0:2 * D].rearrange("p (l d) -> p l d", l=2)

            def load(self, sp, t, table, last=None):
                if last is None and not early(t, 1):
                    sp.wait_ge(self.res_done if self.layer == 0 else self.half, t)
                sp.dma_start(self.buffers(last).x, tile_rows(table, t)).then_inc(self.x_loaded if last is None else last_loaded[self.layer], 16)

            def store(self, sp, t, last=None):
                b = self.buffers(last)
                if self.layer == 0:
                    sp.wait_ge(self.y_copied, t + 1)
                    sp.dma_start(tile_rows(y_dram, t), b.y).then_inc(self.y_stored, 16)
                    sp.wait_ge(self.pre_done, t + 1)
                    sp.dma_start(tile_rows(pre_dram, t), b.pre).then_inc(self.rows_stored, 16)
                    return
                sp.wait_ge(self.norm_done, t + 1)
                if isinstance(t, int) and t == NT - 1:
                    left = N - (NT - 1) * P
                    sp.dma_start(out[N - left:N, :], b.nrm[0:left, :]).then_inc(self.rows_stored, 16)
                else:
                    sp.dma_start(tile_rows(out, t), b.nrm).then_inc(self.rows_stored, 16)

            def stage_sums(self, act, t, last=None, added=None):
                if added is not None:
                    act.wait_ge(*added)
                if last is None and not early(t, 1):
                    act.wait_ge(self.summed, t)
                at, stage = bass.ds(t * P, P), self.buffers(last).stage
                if self.layer == 0:
                    act.activation(stage[:, 0:4, :], acc_a[:, :, at], ACT.Copy)
                else:
                    for rows, part, of, n in ((slice(0, 64), 0, slice(0, 64), 0), (slice(64, 128), 0, slice(64, 128), 1),
                                              (slice(0, 64), 1, slice(64, 128), 2), (slice(64, 128), 1, slice(64, 128), 3)):
                        act.activation(stage[rows, part, :], acc_a[of, n, at], ACT.Copy)
                act.activation(stage[:, (4, 2)[self.layer], :], acc_b[:, at], ACT.Copy).then_inc(self.staged, 1)

            def root(self, act, t, last=None):
                b = self.buffers(last)
                act.wait_ge(self.var_done, t + 1)
                act.activation(b.std, b.mv[:, 1:2], ACT.Sqrt, bias=eps[:]).then_inc(self.std_done, 1)

            def copy_transposed(self, act, t, last=None):
                b = self.buffers(last)
                act.wait_ge(self.transposed, t + 1)
                if last is None and not early(t, 1):
                    act.wait_ge(self.lin_done, t)
                act.activation(b.trn_a, self.trn_bank(last)[:, 0:P], ACT.Copy)
                act.activation(b.trn_b, self.trn_bank(last)[0:MUL1, P:2 * P], ACT.Copy).then_inc(self.trn_copied, 1)

            def copy_y(self, act, t, last=None):
                act.wait_ge(self.lin_done, t + 1)
                if last is None and not early(t, 1):
                    act.wait_ge(self.y_stored, t * 16)
                act.activation(self.buffers(last).y, self.lin_rows(last)[:, 0, :], ACT.Copy,
                               scale=node_attr[:, bass.ds(t, 1)]).then_inc(self.y_copied, 1)

            def sums(self, pe, t, last=None):
                pe.wait_ge(self.staged, t + 1)
                if last in (None, 0) and not early(t, 1):
                    pe.wait_ge(self.half, t)
                w, parts = ((msg_w, 5), (sum_w, 3))[self.layer]
                for n in range(parts):
                    mm = pe.matmul(self.sum_rows(last), self.buffers(last).stage[:, n, :], w[:, n, :], start=(n == 0), stop=(n == parts - 1))
                mm.then_inc(self.summed, 1)

            def transposes(self, pe, t, last=None):
                nrm, bank = self.buffers(last).nrm, self.trn_bank(last)
                pe.wait_ge(self.norm_done, t + 1)
                if last in (None, 0) and not early(t, 1):
                    pe.wait_ge(self.trn_copied, t)
                if last == 2:
                    pe.wait_ge(self.trn_copied, t - 1)
                pe.transpose(bank[:, 0:P], nrm[:, 0:P], ident[:])
                pe.transpose(bank[0:MUL1, P:2 * P], nrm[:, P:D], ident[:]).then_inc(self.transposed, 1)

            def linear(self, pe, t, last=None):
                b, dst = self.buffers(last), self.lin_rows(last)
                pe.wait_ge(self.trn_copied, t + 1)
                if last in (None, 0) and not early(t, 1):
                    pe.wait_ge(self.pre_done, t)
                pe.matmul(dst[:, :, 0:P], b.trn_a, lin_w[:], start=True, stop=True)
                pe.matmul(dst[:, :, P:D], b.trn_b, lin_wz[:], start=True, stop=True).then_inc(self.lin_done, 1)

            def residual(self, dve, t, last=None):
                b, rows = self.buffers(last), self.sum_rows(last)
                dve.wait_ge(self.summed, t + 1)
                if last is None:
                    dve.wait_ge(self.x_loaded, t * 16 + 16)
                    if not early(t, 1):
                        dve.wait_ge(self.norm_done, t)
                else:
                    dve.wait_ge(last_loaded[self.layer], 16 * (NT - NE))
                if self.layer == 0:
                    dve.scalar_tensor_tensor(out=b.res, in0=rows, scalar=0.0, in1=b.x, op0=ALU.max, op1=ALU.add)\
                       .then_inc(self.half, 1)
                    dve.wait_ge(self.half, t + 1)
                    dve.tensor_tensor(b.res, b.res, b.x, ALU.add).then_inc(self.res_done, 1)
                    dve.wait_ge(self.res_done, t + 1)
                else:
                    dve.scalar_tensor_tensor(out=b.res, in0=rows, scalar=node_attr[:, bass.ds(t, 1)], in1=b.x,
                                             op0=ALU.mult, op1=ALU.add).then_inc(self.half, 1)
                    dve.wait_ge(self.half, t + 1)
                dve.bn_stats(b.stats, b.res).then_inc(self.stats_done, 1)

            def variance(self, dve, t, last=None):
                b = self.buffers(last)
                wait_apart(dve, self.stats_done, t + 1)
                dve.bn_aggr(b.mv, b.stats).then_inc(self.var_done, 1)

            def measured(self, dve, t, last=None):
                self.residual(dve, t, last)
                self.variance(dve, t, last)

            def normed(self, dve, t, last=None):
                b = self.buffers(last)
                dve.wait_ge(self.std_done, t + 1)
                dve.reciprocal(b.rstd, b.std).then_inc(self.rstd_done, 1)
                dve.wait_ge(self.rstd_done, t + 1)
                if last is None and not early(t, 1):
                    if self.layer == 0:
                        dve.wait_ge(self.transposed, t)
                        dve.wait_ge(self.pre_done, t)
                    else:
                        dve.wait_ge(self.rows_stored, t * 16)
                dve.tensor_scalar(b.nrm, b.res, b.mv[:, 0:1], b.rstd, ALU.subtract, ALU.mult).then_inc(self.norm_done, 1)

            def self_interaction(self, dve, t, last=None):
                b = self.buffers(last)
                dve.wait_ge(self.y_copied, t + 1)
                if last is None and not early(t, 1):
                    dve.wait_ge(self.rows_stored, t * 16)
                dve.scalar_tensor_tensor(out=b.pre, in0=self.lin_rows(last)[:, 1, :], scalar=node_attr[:, bass.ds(t, 1)], in1=b.nrm,
                                         op0=ALU.mult, op1=ALU.add).then_inc(self.pre_done, 1)

            def on_sync(self, sp, t, table):
                self.load(sp, t, table)
                self.store(sp, t)

            def on_scalar(self, act, t, added=None):
                self.stage_sums(act, t, added=added)
                self.root(act, t)
                if self.layer == 0:
                    self.copy_transposed(act, t)
                    self.copy_y(act, t)

            def on_tensor(self, pe, t):
                self.sums(pe, t)
                if self.layer == 0:
                    self.transposes(pe, t)
                    self.linear(pe, t)

            def on_vector(self, dve, t):
                self.residual(dve, t)
                self.variance(dve, t)
                self.normed(dve, t)
                if self.layer == 0:
                    self.self_interaction(dve, t)

            def all_stored(self, engine, n):
                if self.layer == 0:
                    engine.wait_ge(self.y_stored, 16 * n)
                engine.wait_ge(self.rows_stored, 16 * n)

        class FarEdges:

            def __init__(self, name, layer, table):
                self.layer, self.table = layer, table
                (self.lists_loaded, self.rows_gathered, self.rad_loaded, self.hid_lin, self.hid_out, self.w_out, self.hots,
                 self.window_summed, self.block_done) = (sem(f"{name}_{n}") for n in (
                    "lists_loaded", "rows_gathered", "rad_loaded", "hid_lin", "hid_out", "w_out", "hots", "window_summed", "block_done"))
                self.windows, self.blocks, self.lists = NPAD // FW, U // 2, 2 * ITERS
                lo = K * D
                assert K * 5 * FW <= 4 * K * D
                self.hot = work[:, lo:lo + K * 5 * FW].rearrange("p (k j n) -> p k j n", k=K, j=5)
                lo = 5 * K * D
                self.nodes = work[:, lo:lo + FW]
                self.far_dst = work[:, lo + FW:lo + FW + K]
                self.is_far = work[:, lo + FW + K:lo + FW + 2 * K]
                self.all_dst = work[:, lo + FW + 2 * K:lo + FW + 3 * K].bitcast(I32)

            def lists_in(self, g, b):
                return g * (16 * (self.blocks + 1)) + 16 * (b + 2)

            def on_sync(self, sp):
                with sp.Fori(0, self.lists) as g:
                    for b in range(self.blocks):
                        c = g * self.blocks + b
                        sp.wait_ge(self.block_done, c + 1)
                        if b == 0:
                            sp.dma_start(idx[0][:], a["src"][bass.ds(g, 1)].rearrange("o p t -> (o p) t")).then_inc(self.lists_loaded, 16)
                        sp.dma_start(self.all_dst, a["dst_tiles"][:, bass.ds(c * K, K)]).then_inc(self.lists_loaded, 16)
                        if self.layer == 1:
                            load_radial(sp, rad[0], c, self.rad_loaded)
                        wait_apart(sp, self.lists_loaded, self.lists_in(g, b))
                sp.wait_ge(self.block_done, BLOCKS + 1)

            def on_gpsimd(self, pool):
                with pool.Fori(0, self.lists) as g:
                    for b in range(self.blocks):
                        pool.wait_ge(self.block_done, g * self.blocks + (b + 1))
                        wait_apart(pool, self.lists_loaded, self.lists_in(g, b))
                        for k in range(K):
                            t = b * K + k
                            pool.indirect_dma_start(gat[0][:, k, :], None, self.table, bass.IndirectOffsetOnAxis(idx[0][:, t:t + 1], 0))\
                                .then_inc(self.rows_gathered, 16)
                pool.wait_ge(self.block_done, BLOCKS + 1)

            def on_scalar(self, act):
                with act.Fori(0, BLOCKS) as c:
                    act.wait_ge(self.hid_lin, c + 1)
                    act.activation(hid[0], banks[2][0:NR, 0:BE], ACT.Relu, scale=RELU_SCALE).then_inc(self.hid_out, 1)
                act.wait_ge(self.block_done, BLOCKS + 1)

            def on_tensor(self, pe):
                with pe.Fori(0, BLOCKS) as c:
                    if self.layer == 1:
                        pe.wait_ge(self.rad_loaded, c * 48 + 48)
                        pe.matmul(banks[2][0:NR, 0:BE], fc1[:], rad[0], start=True, stop=True).then_inc(self.hid_lin, 1)
                        pe.wait_ge(self.hid_out, c + 1)
                        for k in range(K):
                            mm = pe.matmul(w_of[0][:, k, 0:NW], hid[0][:, k * P:k * P + P], fc2[:], start=True, stop=True)
                        mm.then_inc(self.w_out, 1)
                    with pe.Fori(0, self.windows) as w:
                        pe.wait_ge(self.hots, c * self.windows + w + 1)
                        block_sums(pe, self.layer, (banks[0], banks[1][:, 0:FW]), (gat, prod)[self.layer][0], self.hot).then_inc(self.window_summed, 1)
                pe.wait_ge(self.block_done, BLOCKS + 1)

            def on_vector(self, dve):
                for n in range(FW // W):
                    dve.tensor_scalar(self.nodes[:, n * W:n * W + W], iota[:], float(n * W + 1), None, ALU.add)
                dve.drain().then_inc(self.block_done, 1)
                with dve.Fori(0, BLOCKS) as c:
                    t = c * K
                    dve.wait_ge(self.rows_gathered, c * (16 * K) + 16 * K)
                    dve.tensor_scalar(self.is_far, rel[:, bass.ds(t, K)], float(W), None, ALU.is_ge)
                    dve.drain()
                    dve.scalar_tensor_tensor(out=self.far_dst, in0=self.all_dst, scalar=1.0, in1=self.is_far, op0=ALU.add, op1=ALU.mult)
                    if self.layer == 1:
                        dve.wait_ge(self.w_out, c + 1)
                        weighted_rows(dve, prod[0], w_of[0], gat[0])
                    dve.drain()
                    with dve.Fori(0, self.windows) as w:
                        dve.tensor_tensor(self.hot[:, :, 0, :], self.nodes.rearrange("p (o n) -> p o n", o=1).to_broadcast([P, K, FW]),
                                          self.far_dst.rearrange("p (k o) -> p k o", o=1).to_broadcast([P, K, FW]), ALU.is_equal)
                        dve.drain()
                        for j in range(4):
                            dve.tensor_tensor(self.hot[:, :, j + 1, :], self.hot[:, :, 0, :],
                                              sh[:, bass.ds(t, K), j:j + 1].to_broadcast([P, K, FW]), ALU.mult)
                        dve.tensor_scalar(self.nodes, self.nodes, float(FW), None, ALU.add)
                        dve.drain().then_inc(self.hots, 1)
                        dve.wait_ge(self.window_summed, c * self.windows + w + 1)
                        at = bass.ds(w * FW, FW)
                        dve.tensor_tensor(acc_a[:, :, at], acc_a[:, :, at], banks[0].rearrange("p (j n) -> p j n", j=4), ALU.add)
                        dve.tensor_tensor(acc_b[:, at], acc_b[:, at], banks[1][:, 0:FW], ALU.add)
                        dve.drain()
                    dve.tensor_scalar(self.nodes, self.nodes, float(-FW * self.windows), None, ALU.add)
                    dve.drain().then_inc(self.block_done, 1)

        nodes0, nodes1 = Node("nodes0", 0), Node("nodes1", 1)
        LAST = list(range(NE, NT))
        last_loaded = [sem("last_x_loaded"), sem("last_pre_loaded")]

        def staggered(engine, *steps):
            for m in range(len(LAST) + len(steps) - 1):
                for behind, step in enumerate(steps):
                    if 0 <= m - behind < len(LAST):
                        step(engine, LAST[m - behind], m - behind)

        dst_loaded, rel_loaded, tables_loaded, weights_loaded, places_loaded = (
            sem(n) for n in ("dst_loaded", "rel_loaded", "tables_loaded", "weights_loaded", "places_loaded"))
        places_zeroed, zeros_set, acc_zeroed = (sem(n) for n in ("places_zeroed", "zeros_set", "acc_zeroed"))
        iotas_set, ident_set = sem("iotas_set"), sem("ident_set")
        mins_found, bases_found, margins_found, bases_stored, bases_loaded = (
            sem(n) for n in ("mins_found", "bases_found", "margins_found", "bases_stored", "bases_loaded"))
        rel_found, far_found, measures_stored, measures_loaded, extremes_found, flags_found, flags_set = (
            sem(n) for n in ("rel_found", "far_found", "measures_stored", "measures_loaded", "extremes_found", "flags_found", "flags_set"))
        sh_soon_loaded, sh_rest_loaded, rel_all_found = sem("sh_soon_loaded"), sem("sh_rest_loaded"), sem("rel_all_found")
        products_done, weights_scaled = sem("products_done"), sem("weights_scaled")
        idx_loaded = [[sem(f"idx{h}_loaded{n}") for h in range(2)] for n in range(2)]
        gathered = [[sem(f"gathered{n}_{s}") for s in range(U)] for n in range(2)]
        onehot_built, summed, added = ([sem(f"{m}{n}") for n in range(2)] for m in ("onehot_built", "summed", "added"))
        operands_ready = sem("operands_ready")
        rad_loaded = [sem(f"rad_loaded{s}") for s in range(U)]
        hid_lin_done, hid_done, w_done, z_ready = (sem(n) for n in ("hid_lin_done", "hid_done", "w_done", "z_ready"))
        rad_split, fc1_split = ([sem(f"{name}_split{m}") for m in range(4)] for name in ("rad", "fc1"))
        rad_in_loaded, rad_stored, fc1_in_loaded, fc1_stored = (
            sem(n) for n in ("rad_in_loaded", "rad_stored", "fc1_in_loaded", "fc1_stored"))
        zeroed1, zeroed1_dma = sem("zeroed1"), sem("zeroed1_dma")

        used[0] = shared0
        room = carve(max(U * BE, BLOCKS))
        dst_rows = room[0:ITERS, 0:U * BE].rearrange("p (b e) -> p b e", b=U)
        base_b = room[:, 0:BLOCKS].bitcast(I32)
        bmin, bmin_i, floors = carve(U, ITERS), carve(U, ITERS).bitcast(I32), carve(1, ITERS)
        least, margin, far = carve(1, ITERS), carve(1, ITERS), carve(1)
        far_row, margin_row = carve(P, 1), carve(ITERS, 1)
        extremes, found_flags = carve(2, 1), carve(4, 1)
        used[0] = prod0
        w1t, ws, w2t = carve(64, 64), carve(64, 64), carve(128, 64)
        w3t, wv, w4t, w5t = carve(64, 32), carve(32, 32), carve(128, 32), carve(128, 32)
        fc1_in, fc1_rest = carve(NR, NB), carve(NR, NB)
        fc1_parts = carve(3 * NR // 2, NB).bitcast(BF16).rearrange("p (m n) -> p m n", m=3)
        PLACES = 16 * 16
        TABLES = 8 * 16
        SOON = 4 * U * K
        HALF = NT // 2 * P

        def zeros_over(n):
            return zeros[:].rearrange("p (r n) -> p r n", r=1).to_broadcast([P, n, P])

        def in_tiles(t):
            return t.rearrange("p (r n) -> p r n", n=P)

        far0 = FarEdges("far0", 0, a["x"])
        far1 = FarEdges("far1", 1, y_dram)

        with nc.Block() as block:
            @block.sync
            def _(sp):
                for h in range(2):
                    sp.dma_start(idx[h][:], a["src"][h]).then_inc(idx_loaded[0][h], 16)
                sp.dma_start(dst_rows.bitcast(I32), a["dst"].rearrange("(p b e) -> p b e", p=ITERS, b=U)).then_inc(dst_loaded, 16)
                sp.dma_start(rel[:].bitcast(I32), a["dst_tiles"]).then_inc(rel_loaded, 16)
                sp.dma_start(sh[:, 0:SOON], a["sh"][:, 0:SOON]).then_inc(sh_soon_loaded, 16)
                def radial_in(i):
                    sp.dma_start(rad_in, a["radial"][bass.ds(i * U, U)].rearrange("c b e -> (c b e)").rearrange("(p n) -> p n", n=RN)).then_inc(rad_in_loaded, 16)

                def radial_out(i):
                    sp.wait_ge(rad_split[3], i + 1)
                    for m in range(3):
                        sp.dma_start(rad_dram[bass.ds(i * U, U), m].rearrange("c b e -> c (b e)").rearrange("c (r n) -> c r n", n=RN),
                                     rad_parts[:, m, :]).then_inc(rad_stored, 16)

                sp.wait_ge(bases_found, 1)
                sp.dma_start(base_dram.rearrange("(p b) -> p b", p=ITERS), bmin_i).then_inc(bases_stored, 16)
                sp.wait_ge(bases_stored, 16)
                sp.dma_start(base_b, base_dram.rearrange("(o b) -> o b", o=1).to_broadcast([P, BLOCKS])).then_inc(bases_loaded, 16)
                sp.dma_start(base_row[:], base_dram.rearrange("(o b) -> o b", o=1)).then_inc(bases_loaded, 16)
                radial_in(0)
                sp.dma_start(sh[:, SOON:], a["sh"][:, SOON:]).then_inc(sh_rest_loaded, 16)

                def body(i, first, last, tile):
                    if not last:
                        refill_indices(sp, i, 0, idx_loaded[0], gathered[0])
                    if tile is not None:
                        if not early(tile, 1):
                            nodes0.store(sp, tile - 1)
                        nodes0.load(sp, tile, a["x"])
                    if not last:
                        refill_indices(sp, i, 1, idx_loaded[0], gathered[0])
                    radial_out(i)
                    if not last:
                        radial_in(i + 1)
                    if last and tile is not None:
                        nodes0.store(sp, tile)
                found = iterations(sp, body)
                is_far, late, _ = found
                for s in range(U):
                    sp.wait_ge(gathered[0][s], ITERS * 16 * K)
                with sp.If(is_far):
                    sp.wait_ge(added[0], BLOCKS)
                    far0.on_sync(sp)
                with sp.If(late):
                    nodes0.on_sync(sp, 0, a["x"])
                    with sp.Fori(1, NE) as t:
                        nodes0.on_sync(sp, t, a["x"])
                for h in range(2):
                    sp.dma_start(idx[h][:], a["src"][h]).then_inc(idx_loaded[1][h], 16)
                sp.wait_ge(summed[0], BLOCKS)
                for n, t in enumerate(LAST):
                    nodes0.load(sp, t, a["x"], n)
                for n, t in enumerate(LAST):
                    nodes0.store(sp, t, n)
                nodes0.all_stored(sp, NT)

                sp.wait_ge(rad_stored, 48 * ITERS)
                for q in range(U):
                    load_radial(sp, rad[q], q, rad_loaded[q])

                def body(i, first, last, tile):
                    for q in range(U):
                        if not (first and q < 3) and not (last and q >= 3):
                            sp.wait_ge(hid_lin_done, i * U + (q - 2))
                            load_radial(sp, rad[(q + 3) % U], i * U + (q + 3), rad_loaded[(q + 3) % U])
                        if q % 3 == 2 and not last:
                            refill_indices(sp, i, q // 3, idx_loaded[1], gathered[1])
                        if q == 2 and tile is not None:
                            if not early(tile, 1):
                                nodes1.store(sp, tile - 1)
                            nodes1.load(sp, tile, pre_dram)
                    if last and tile is not None:
                        nodes1.store(sp, tile)
                iterations(sp, body, found)
                with sp.If(is_far):
                    sp.wait_ge(added[1], BLOCKS)
                    far1.on_sync(sp)
                with sp.If(late):
                    nodes1.on_sync(sp, 0, pre_dram)
                    with sp.Fori(1, NE) as t:
                        nodes1.on_sync(sp, t, pre_dram)
                sp.wait_ge(summed[1], BLOCKS)
                for n, t in enumerate(LAST):
                    nodes1.load(sp, t, pre_dram, n)
                for n, t in enumerate(LAST):
                    nodes1.store(sp, t, n)
                nodes1.all_stored(sp, NT)

            @block.gpsimd
            def _(pool):
                pool.iota(iota[:], [[1, W]], base=0, channel_multiplier=0, allow_small_or_imprecise_dtypes=True)
                pool.iota(floors, [[0, 1]], base=-P * (EARLY - 1), channel_multiplier=P,
                          allow_small_or_imprecise_dtypes=True).then_inc(iotas_set, 1)
                pool.memset(ident[:], 0.0).then_inc(ident_set, 1)
                pool.wait_ge(ident_set, 1)
                pool.affine_select(out=ident[:], in_=ident[:], compare_op=ALU.not_equal, fill=1.0, base=0,
                                   pattern=[[-1, P]], channel_multiplier=1).then_inc(ident_set, 1)

                def body(i, first, last, tile):
                    for q in range(U):
                        gather_block(pool, i, q, first, a["x"], idx_loaded[0], gathered[0], summed[0])
                found = iterations(pool, body)
                is_far, late, _ = found
                with pool.If(is_far):
                    pool.wait_ge(added[0], BLOCKS)
                    far0.on_gpsimd(pool)
                pool.wait_ge(nodes0.staged, NT)
                pool.memset(acc_b[:], 0.0).then_inc(zeroed1, 1)
                nodes0.all_stored(pool, NT)

                def body(i, first, last, tile):
                    for q in range(U):
                        gather_block(pool, i, q, first, y_dram, idx_loaded[1], gathered[1], summed[1])
                iterations(pool, body, found)
                with pool.If(is_far):
                    pool.wait_ge(added[1], BLOCKS)
                    far1.on_gpsimd(pool)

            @block.scalar
            def _(act):
                act.preload_act_table(ACT.Sqrt)
                act.wait_ge(zeros_set, 1)
                for part in (0, 1, 2):
                    act.activation(in_tiles(acc_a[:, part, :]), zeros_over(NT), ACT.Copy)
                act.activation(in_tiles(acc_b[:, HALF:]), zeros_over(NT - NT // 2), ACT.Copy).then_inc(acc_zeroed, 1)
                for dst, src in ((w1t, "W1t"), (ws, "Ws"), (w3t, "W3t"), (wv, "Wv")):
                    act.dma_start(dst, a[src]).then_inc(weights_loaded, 16)
                for r in range(4):
                    for dst, src in ((w2t, "W2t"), (w4t, "W4t"), (w5t, "W5t")):
                        act.dma_start(dst[:, 32 * r:32 * r + 32], a[src]).then_inc(weights_loaded, 16)
                act.dma_start(node_attr[:], a["node_attr"]).then_inc(tables_loaded, 16)
                act.dma_start(fc1_in, a["fc1"]).then_inc(fc1_in_loaded, 16)
                act.dma_start(fc2[:], a["fc2"]).then_inc(tables_loaded, 16)
                act.wait_ge(places_zeroed, 1)
                for n, (s, v) in enumerate((("W_l1_0", "W_l1_1"), ("W_si0", "W_si1"))):
                    act.dma_start(lin_w[0:64, n, 0:64], a[s]).then_inc(places_loaded, 16)
                    act.dma_start(lin_w[64:96, n, 64:96], a[v]).then_inc(places_loaded, 16)
                    act.dma_start(lin_w[96:128, n, 96:128], a[v]).then_inc(places_loaded, 16)
                    act.dma_start(lin_wz[:, n, :], a[v]).then_inc(places_loaded, 16)
                act.dma_start(sum_w[0:64, 0, 0:64], a["W_l2_00"]).then_inc(places_loaded, 16)
                for i in range(3):
                    lo = MUL0 + MUL1 * i
                    rows, part = ((slice(64, 128), 0), (slice(0, 64), 1), (slice(64, 128), 1))[i]
                    act.dma_start(sum_w[rows, part, lo:lo + 32], a["W_l2_01"]).then_inc(places_loaded, 16)
                    act.dma_start(sum_w[32 * i:32 * i + 32, 2, lo:lo + 32], a["W_l2_11"]).then_inc(places_loaded, 16)
                act.dma_start(sum_w[96:128, 2, 0:64], a["W_l2_10"]).then_inc(places_loaded, 16)
                act.wait_ge(fc1_split[3], 1)
                act.dma_start(fc1_dram.rearrange("m b h -> b m h"), fc1_parts).then_inc(fc1_stored, 16)
                act.wait_ge(fc1_stored, 16)
                for rows, m in enumerate((0, 0, 0, 1, 1, 2)):
                    act.dma_start(fc1[rows * NB:rows * NB + NB, :], fc1_dram[m]).then_inc(tables_loaded, 16)
                act.wait_ge(margins_found, 1)
                act.wait_ge(far_found, 1)
                act.dma_start(measures_dram[0].rearrange("(p o) -> p o", o=1), far).then_inc(measures_stored, 16)
                act.dma_start(measures_dram[1, 0:ITERS].rearrange("(p o) -> p o", o=1), margin).then_inc(measures_stored, 16)
                act.wait_ge(measures_stored, 32)
                act.dma_start(far_row, measures_dram[0].rearrange("(o p) -> o p", o=1)).then_inc(measures_loaded, 16)
                act.dma_start(margin_row, measures_dram[1, 0:ITERS].rearrange("(o p) -> o p", o=1)).then_inc(measures_loaded, 16)
                act.wait_ge(products_done, 1)
                act.wait_ge(places_zeroed, 1)
                g1, g2, g3, g4, g5 = banks[2:7]
                c2, c5 = C0 * INV3 * LIN_S, C1 * INV6 * LIN_V
                c34 = C1 * INV3 * LIN_V
                v0, v1, j = slice(64, 96), slice(96, 128), [slice(32 * q, 32 * q + 32) for q in range(4)]
                s_, hs, hv = slice(0, 64), slice(0, 64), [slice(64 + 32 * i, 96 + 32 * i) for i in range(3)]
                places = [
                    (0, s_, hs, g1, C0 * LIN_S), (0, v0, hv[0], g4, c34), (0, v1, hv[1], g4, c34),
                    (1, s_, hv[0], g3, c34), (1, v0, hs, g2, c2), (1, v1, hv[2], g5, -c5),
                    (2, s_, hv[1], g3, c34), (2, v0, hv[2], g5, c5), (2, v1, hs, g2, c2),
                    (3, s_, hv[2], g3, c34), (3, v0, hv[1], g5, -c5), (3, v1, hv[0], g5, c5),
                    (4, j[0], hv[2], g4, c34), (4, j[1], hv[1], g5, c5), (4, j[2], hv[0], g5, -c5), (4, j[3], hs, g2, c2),
                ]
                for part, rows, cols, g, c in places:
                    act.activation(msg_w[rows, part, cols], g[rows, 0:cols.stop - cols.start], ACT.Copy, scale=float(c))
                act.wait_ge(places_loaded, PLACES)
                act.activation(lin_w[0:64], lin_w[0:64], ACT.Copy, scale=float(LIN_S))
                act.activation(lin_w[64:128], lin_w[64:128], ACT.Copy, scale=float(LIN_V))
                act.activation(lin_wz[:], lin_wz[:], ACT.Copy, scale=float(LIN_V))
                act.activation(sum_w[:], sum_w[:], ACT.Copy, scale=SUM_SCALE).then_inc(weights_scaled, 1)
                act.wait_ge(weights_scaled, 1)
                act.activation(sum_w[96:128, 2, 0:64], sum_w[96:128, 2, 0:64], ACT.Copy, scale=float(INV3)).then_inc(weights_scaled, 1)
                act.wait_ge(weights_scaled, 2)
                act.wait_ge(tables_loaded, TABLES)

                found = load_flags(act)
                is_far, late, in_order = found
                with act.If(in_order):
                    nodes0.on_scalar(act, 0, added=(added[0], EARLY * U))
                    with act.Fori(1, NE) as t:
                        nodes0.on_scalar(act, t, added=(added[0], t * U + EARLY * U))
                with act.If(is_far):
                    act.wait_ge(far0.block_done, BLOCKS + 1)
                with act.If(late):
                    act.wait_ge(added[0], BLOCKS)
                    nodes0.on_scalar(act, 0)
                    with act.Fori(1, NE) as t:
                        nodes0.on_scalar(act, t)
                for n, t in enumerate(LAST):
                    nodes0.stage_sums(act, t, n, (added[0], BLOCKS))
                act.wait_ge(nodes0.staged, NT)
                act.dma_start(in_tiles(acc_a[:, 0, :]), zeros_over(NT)).then_inc(zeroed1_dma, 16)
                staggered(act, nodes0.root, nodes0.copy_transposed, nodes0.copy_y)
                act.activation(in_tiles(acc_a[:, 1, :]), zeros_over(NT), ACT.Copy).then_inc(zeroed1, 1)

                def relu(c, s):
                    act.wait_ge(hid_lin_done, c + 1)
                    if not early(c, 2):
                        act.wait_ge(w_done, c - 1)
                    act.activation(hid[s], banks[2][0:NR, 0:BE], ACT.Relu, scale=RELU_SCALE).then_inc(hid_done, 1)

                relu(0, 0)

                def body(i, first, last, tile):
                    for q in range(U):
                        c, s = i * U + q, q % 2
                        if not (last and q == U - 1):
                            relu(c + 1, 1 - s)
                        if tile is not None and q == 1:
                            nodes1.stage_sums(act, tile, added=(added[1], i * U))
                        if tile is not None and q == 4:
                            nodes1.root(act, tile)
                iterations(act, body, found)
                with act.If(is_far):
                    act.wait_ge(added[1], BLOCKS)
                    far1.on_scalar(act)
                with act.If(late):
                    act.wait_ge(added[1], BLOCKS)
                    nodes1.on_scalar(act, 0)
                    with act.Fori(1, NE) as t:
                        nodes1.on_scalar(act, t)
                for n, t in enumerate(LAST):
                    nodes1.stage_sums(act, t, n, (added[1], BLOCKS))
                staggered(act, nodes1.root)

            @block.tensor
            def _(pe):
                def weight_products():
                    pe.wait_ge(weights_loaded, 16 * 16)
                    pe.matmul(banks[2][0:64, 0:64], w1t, ws, start=True, stop=True)
                    pe.matmul(banks[3][:, 0:64], w2t, ws, start=True, stop=True)
                    pe.matmul(banks[4][0:64, 0:32], w3t, wv, start=True, stop=True)
                    pe.matmul(banks[5][:, 0:32], w4t, wv, start=True, stop=True)
                    pe.matmul(banks[6][:, 0:32], w5t, wv, start=True, stop=True).then_inc(products_done, 1)
                    pe.wait_ge(ident_set, 2)

                def body(i, first, last, tile):
                    for q in range(U):
                        c, s = i * U + q, q % 2
                        pe.wait_ge(operands_ready, c + 1)
                        if not early(c, 2):
                            pe.wait_ge(added[0], c - 1)
                        pe.wait_ge(gathered[0][q], i * (16 * K) + 16 * K)
                        block_sums(pe, 0, sum_bank(s), gat[q], hot[s]).then_inc(summed[0], 1)
                        if tile is not None:
                            if q == 1:
                                nodes0.sums(pe, tile)
                            if q == 3:
                                nodes0.transposes(pe, tile)
                            if q == 4:
                                nodes0.linear(pe, tile)
                    if first:
                        weight_products()
                found = iterations(pe, body)
                is_far, late, _ = found
                with pe.If(is_far):
                    far0.on_tensor(pe)
                with pe.If(late):
                    nodes0.on_tensor(pe, 0)
                    with pe.Fori(1, NE) as t:
                        nodes0.on_tensor(pe, t)
                staggered(pe, nodes0.sums, nodes0.transposes, nodes0.linear)

                def hidden(c, q, uses):
                    pe.wait_ge(rad_loaded[q], uses * 48)
                    if not early(c, 1):
                        pe.wait_ge(hid_done, c)
                    pe.matmul(banks[2][0:NR, 0:BE], fc1[:], rad[q], start=True, stop=True).then_inc(hid_lin_done, 1)

                def sums(c, s):
                    pe.wait_ge(z_ready, c + 1)
                    if not early(c, 2):
                        pe.wait_ge(added[1], c - 1)
                    block_sums(pe, 1, sum_bank(s), prod[s], hot[s]).then_inc(summed[1], 1)

                hidden(0, 0, 1)

                def body(i, first, last, tile):
                    for q in range(U):
                        c, s = i * U + q, q % 2
                        if not (last and q == U - 1):
                            hidden(c + 1, (q + 1) % U, i + 1 + (q + 1) // U)
                        pe.wait_ge(hid_done, c + 1)
                        if not early(c, 2):
                            pe.wait_ge(z_ready, c - 1)
                        for k in range(K):
                            mm = pe.matmul(w_of[s][:, k, 0:NW], hid[s][:, k * P:k * P + P], fc2[:], start=True, stop=True)
                        mm.then_inc(w_done, 1)
                        if not early(c, 1):
                            sums(c - 1, 1 - s)
                        if tile is not None and q == 3:
                            nodes1.sums(pe, tile)
                iterations(pe, body, found)
                sums(BLOCKS - 1, 1)
                with pe.If(is_far):
                    pe.wait_ge(added[1], BLOCKS)
                    far1.on_tensor(pe)
                with pe.If(late):
                    nodes1.on_tensor(pe, 0)
                    with pe.Fori(1, NE) as t:
                        nodes1.on_tensor(pe, t)
                staggered(pe, nodes1.sums)

            @block.vector
            def _(dve):
                dve.memset(zeros[:], 0.0).then_inc(zeros_set, 1)
                dve.memset(lin_w[:], 0.0)
                dve.memset(sum_w[:], 0.0)
                dve.memset(msg_w[:], 0.0)
                dve.memset(eps[:], EPS).then_inc(places_zeroed, 1)
                dve.memset(acc_b[:, 0:HALF], 0.0)
                dve.wait_ge(dst_loaded, 16)
                dve.tensor_reduce(bmin, dst_rows.bitcast(I32), AX.X, ALU.min).then_inc(mins_found, 1)
                dve.wait_ge(mins_found, 1)
                dve.tensor_scalar(bmin_i, bmin, float(NPAD - W), None, ALU.min).then_inc(bases_found, 1)
                dve.wait_ge(bases_found, 1)
                dve.tensor_reduce(least, bmin_i, AX.X, ALU.min).then_inc(mins_found, 1)
                dve.wait_ge(mins_found, 2)
                dve.wait_ge(iotas_set, 1)
                dve.tensor_tensor(margin, least, floors, ALU.subtract).then_inc(margins_found, 1)
                dve.memset(acc_a[:, 3, :], 0.0)
                dve.wait_ge(rel_loaded, 16)
                dve.wait_ge(bases_loaded, 32)

                def relative(lo, hi):
                    d = rel[:, lo * K:hi * K].rearrange("p (b k) -> p b k", k=K)
                    return dve.tensor_tensor(d, d.bitcast(I32), base_b[:, lo:hi].rearrange("p (b o) -> p b o", o=1)
                                             .to_broadcast([P, hi - lo, K]), ALU.subtract)

                relative(0, U).then_inc(rel_found, 1)
                dve.wait_ge(rel_found, 1)
                dve.wait_ge(sh_soon_loaded, 16)

                def after_first():
                    relative(U, BLOCKS).then_inc(rel_all_found, 1)
                    dve.wait_ge(rel_all_found, 1)
                    dve.tensor_reduce(far, rel[:], AX.X, ALU.max).then_inc(far_found, 1)
                    dve.wait_ge(fc1_in_loaded, 16)
                    for m in range(4):
                        split(dve, fc1_in, fc1_rest, fc1_parts, fc1_split, m, 1)
                    dve.wait_ge(sh_rest_loaded, 16)

                def set_flags():
                    dve.wait_ge(tables_loaded, TABLES)
                    dve.wait_ge(measures_loaded, 32)
                    dve.tensor_reduce(extremes[:, 0:1], far_row, AX.X, ALU.max)
                    dve.tensor_reduce(extremes[:, 1:2], margin_row, AX.X, ALU.min).then_inc(extremes_found, 1)
                    dve.wait_ge(extremes_found, 1)
                    dve.tensor_scalar(found_flags[:, 0:1], extremes[:, 0:1], float(W), None, ALU.is_ge)
                    dve.tensor_scalar(found_flags[:, 1:2], extremes[:, 1:2], 0.0, None, ALU.is_lt)
                    dve.tensor_scalar(found_flags[:, 2:3], extremes[:, 0:1], float(W), None, ALU.is_lt)
                    dve.tensor_scalar(found_flags[:, 3:4], extremes[:, 1:2], 0.0, None, ALU.is_ge).then_inc(flags_found, 1)
                    dve.wait_ge(flags_found, 1)
                    dve.tensor_copy(flags[:, 0:1], found_flags[:, 0:1])
                    dve.tensor_tensor(flags[:, 1:2], found_flags[:, 0:1], found_flags[:, 1:2], ALU.max)
                    dve.tensor_tensor(flags[:, 2:3], found_flags[:, 2:3], found_flags[:, 3:4], ALU.min).then_inc(flags_set, 1)

                def body(i, first, last, tile):
                    for q in range(U):
                        c, s = i * U + q, q % 2
                        t = i * (U * K) + q * K
                        if not early(c, 2):
                            dve.wait_ge(summed[0], c - 1)
                        onehots(dve, hot[s], t).then_inc(onehot_built[0], 1)
                        scaled_onehots(dve, hot[s], t, onehot_built[0], c).then_inc(operands_ready, 1)
                        if q == 0:
                            bases = load_bases(0, U - 1) if first else load_bases(i * U - 1, U)
                        if early(c, 2) and q == 1:
                            dve.wait_ge(acc_zeroed, 1)
                        if tile is not None and q == 3:
                            nodes0.normed(dve, tile)
                        if q == 1:
                            dve.wait_ge(rad_in_loaded, i * 16 + 16)
                            if not first:
                                dve.wait_ge(rad_stored, i * 48)
                        if 1 <= q <= 4:
                            split(dve, rad_in, rad_rest, rad_parts, rad_split, q - 1, i + 1)
                        if not early(c, 1):
                            add_sums(dve, c, banks[1 - s], bases[q - first], summed[0], added[0])
                        if tile is not None:
                            if q == 2:
                                nodes0.residual(dve, tile)
                                nodes0.variance(dve, tile)
                            if q == 5:
                                nodes0.self_interaction(dve, tile)
                    if first:
                        after_first()
                    if last:
                        add_sums(dve, BLOCKS, banks[1], load_bases(BLOCKS - 1, 1)[0], summed[0], added[0])
                found = iterations(dve, body, before_flags=set_flags)
                is_far, late, _ = found
                with dve.If(is_far):
                    far0.on_vector(dve)
                with dve.If(late):
                    nodes0.on_vector(dve, 0)
                    with dve.Fori(1, NE) as t:
                        nodes0.on_vector(dve, t)
                staggered(dve, nodes0.measured, nodes0.normed, nodes0.self_interaction)

                for part in (2, 3):
                    dve.memset(acc_a[:, part, :], 0.0)

                def body(i, first, last, tile):
                    for q in range(U):
                        c, s = i * U + q, q % 2
                        t = i * (U * K) + q * K
                        if not early(c, 2):
                            dve.wait_ge(summed[1], c - 1)
                        onehots(dve, hot[s], t).then_inc(onehot_built[1], 1)
                        scaled_onehots(dve, hot[s], t, onehot_built[1], c)
                        if q == 0:
                            bases = load_bases(0, U - 1) if first else load_bases(i * U - 1, U)
                        dve.wait_ge(gathered[1][q], i * (16 * K) + 16 * K)
                        dve.wait_ge(w_done, c + 1)
                        weighted_rows(dve, prod[s], w_of[s], gat[q]).then_inc(z_ready, 1)
                        if early(c, 2) and q == 1:
                            dve.wait_ge(zeroed1, 2)
                            dve.wait_ge(zeroed1_dma, 16)
                        if not early(c, 1):
                            add_sums(dve, c, banks[1 - s], bases[q - first], summed[1], added[1])
                        if tile is not None:
                            if q == 4:
                                nodes1.residual(dve, tile)
                                nodes1.variance(dve, tile)
                            if q == 5:
                                nodes1.normed(dve, tile)
                    if last:
                        add_sums(dve, BLOCKS, banks[1], load_bases(BLOCKS - 1, 1)[0], summed[1], added[1])
                iterations(dve, body, found)
                with dve.If(is_far):
                    far1.on_vector(dve)
                with dve.If(late):
                    nodes1.on_vector(dve, 0)
                    with dve.Fori(1, NE) as t:
                        nodes1.on_vector(dve, t)
                staggered(dve, nodes1.measured, nodes1.normed)


def kernel(**inputs):
    import concourse.bacc as _bacc
    from concourse.bass_utils import run_bass_kernel_spmd as _run

    arr = {k: np.asarray(v) for k, v in inputs.items()}
    order = np.concatenate([np.arange(MUL0), (MUL0 + 3 * np.arange(MUL1)[None, :] + np.arange(3)[:, None]).reshape(-1)])
    back = np.argsort(order)

    def edges(v, fill=0):
        return np.concatenate([v, np.full((EPAD - E,) + v.shape[1:], fill, v.dtype)])

    def by_tile(v):
        return np.ascontiguousarray(v.reshape((TILES, P) + v.shape[1:]).swapaxes(0, 1))

    dst, src = edges(arr["dst"], N - 1), edges(arr["src"])
    nodes = {"x": arr["x"][:, order], "node_attr": arr["node_vec1"]}
    nodes = {k: np.concatenate([v, np.zeros((NPAD - N,) + v.shape[1:], v.dtype)]) for k, v in nodes.items()}
    arrays = {
        "x": nodes["x"],
        "node_attr": nodes["node_attr"].reshape(NT, P).T,
        "dst": dst, "dst_tiles": by_tile(dst),
        "src": src.reshape(2 * ITERS, H, P).swapaxes(1, 2),
        "sh": by_tile(edges(arr["edge_attr_4"])),
        "radial": edges(arr["edge_attr_10"]).reshape(BLOCKS, BE, NB).swapaxes(1, 2),
        "W1t": arr["L0_gnn_W1"].T, "W2t": arr["L0_gnn_W2"].T, "W3t": arr["L0_gnn_W3"].T,
        "W4t": arr["L0_gnn_W4"].T, "W5t": arr["L0_gnn_W5"].T, "Ws": arr["L0_gnn_Ws"], "Wv": arr["L0_gnn_Wv"],
        "fc1": arr["L1_gnn_W_fc1"], "fc2": arr["L1_gnn_W_fc2"],
    }
    for k in ("W_si0", "W_si1", "W_l1_0", "W_l1_1", "W_l2_00", "W_l2_10", "W_l2_01", "W_l2_11"):
        arrays[k] = arr["L1_gnn_" + k]
    arrays = {k: np.ascontiguousarray(v) for k, v in arrays.items()}
    nc = _bacc.Bacc("TRN2", target_bir_lowering=False, num_devices=1)
    args = {k: nc.dram_tensor("in_" + k, v.shape, mybir.dt.from_np(v.dtype), kind="ExternalInput").ap() for k, v in arrays.items()}
    out = nc.dram_tensor("out_rows", (N, D), F32, kind="ExternalOutput").ap()
    build(nc, args, out)
    r = _run(nc, [{"in_" + k: v for k, v in arrays.items()}], core_ids=[0])
    return r.results[0]["out_rows"][:, back]
```
